# Optimizing a Trainium2 kernel written in Bass

```python
import numpy as np
import jax
import jax.numpy as jnp

def _softmax(x, axis=-1):
    return jax.nn.softmax(x, axis=axis)

def _gelu(x):
    return jax.nn.gelu(x, approximate=True)

def _silu(x):
    return jax.nn.silu(x)

def _sigmoid(x):
    return jax.nn.sigmoid(x)

def _layernorm(x, axis=-1, eps=1e-05):
    m = jnp.mean(x, axis=axis, keepdims=True)
    v = jnp.var(x, axis=axis, keepdims=True)
    return (x - m) / jnp.sqrt(v + eps)

def _scatter_add(tgt, idx, src, axis=0):
    return tgt.at[idx].add(src)

def _segment_sum(src, seg, n):
    return jax.ops.segment_sum(src, seg, n)
kernel_name = 'mk_xattn_seq_d1_seqx_r8_24beea'

def setup_inputs(seed: int=0):
    np.random.seed(seed)
    _w = jnp.asarray

    def _rec_inputs():
        import jax
        import jax.numpy as jnp
        _rk = jax.random.key(seed)
        x = -0.000719 + 1.001 * jax.random.normal(jax.random.fold_in(_rk, 1), (4, 256, 160), jnp.float32)
        _lenS = 256 - jax.random.randint(jax.random.fold_in(_rk, 7), (4,), 0, max(1, 256 // 4) + 1, jnp.int32)
        _lenS2 = 1601 - jax.random.randint(jax.random.fold_in(_rk, 8), (4,), 0, max(1, 1601 // 4) + 1, jnp.int32)
        _ctx_2048P = jax.random.normal(jax.random.fold_in(_rk, 11), (4, 16, 256), jnp.float32)
        _ctx_2048c = jax.random.dirichlet(jax.random.fold_in(_rk, 511), 0.3 * jnp.ones((16,), jnp.float32), (4, 1601))
        _ctx_2048t = jnp.einsum('bsk,bkd->bsd', _ctx_2048c, _ctx_2048P)
        _ctx_2048t = _ctx_2048t * jax.lax.rsqrt(jnp.mean(jnp.square(_ctx_2048t)) + 1e-12) * 0.953939
        ctx_2048 = 0.00257118 + 0.99863 * (_ctx_2048t + 0.3 * jax.random.normal(jax.random.fold_in(_rk, 611), (4, 1601, 256), jnp.float32))
        fside_S_0 = jax.random.uniform(jax.random.fold_in(_rk, 12), (256,), jnp.float32, 0.0, 0.999706)
        return (x, ctx_2048, fside_S_0)
    x, ctx_2048, fside_S_0 = _rec_inputs()

    def _L0_xattn_setup():
        import jax, jax.numpy as jnp
        import numpy as np
        HEADS = 20
        NUM_TOKENS = 4
        IP_SCALE = 1.0
        SEM_SCALE = 0.5
        RESCALE = 1.0
        EPS = 1e-12

        def _l2norm(x, axis=-1):
            n = jnp.sqrt(jnp.sum(x * x, axis=axis, keepdims=True))
            return x / jnp.maximum(n, EPS)
        key = jax.random.key(seed)
        ks = jax.random.split(key, 10)
        B, S, C = (2, 128, 160)
        T, E = (81, 256)
        inp = {'hidden_states': jax.random.normal(ks[0], (B, S, C), jnp.float32), 'encoder_hidden_states': jax.random.normal(ks[1], (B, T, E), jnp.float32), 'spatial_mask': jax.random.uniform(ks[2], (S,), jnp.float32), 'W_q': jax.random.normal(ks[3], (C, C), jnp.float32) * C ** (-0.5), 'W_k': jax.random.normal(ks[4], (E, C), jnp.float32) * E ** (-0.5), 'W_v': jax.random.normal(ks[5], (E, C), jnp.float32) * E ** (-0.5), 'W_k_ip': jax.random.normal(ks[6], (E, C), jnp.float32) * E ** (-0.5), 'W_v_ip': jax.random.normal(ks[7], (E, C), jnp.float32) * E ** (-0.5), 'W_out': jax.random.normal(ks[8], (C, C), jnp.float32) * C ** (-0.5), 'b_out': jnp.zeros((C,), jnp.float32)}
        return inp
    _L0_xattn_all = _L0_xattn_setup()
    _L0_xattn_in = {k: v for k, v in _L0_xattn_all.items() if k in ('W_q', 'W_k', 'W_v', 'W_k_ip', 'W_v_ip', 'W_out', 'b_out')}
    del _L0_xattn_all
    return {'x': x, 'ctx_2048': ctx_2048, 'fside_S_0': fside_S_0, 'L0_xattn_W_q': _L0_xattn_in['W_q'], 'L0_xattn_W_k': _L0_xattn_in['W_k'], 'L0_xattn_W_v': _L0_xattn_in['W_v'], 'L0_xattn_W_k_ip': _L0_xattn_in['W_k_ip'], 'L0_xattn_W_v_ip': _L0_xattn_in['W_v_ip'], 'L0_xattn_W_out': _L0_xattn_in['W_out'], 'L0_xattn_b_out': _L0_xattn_in['b_out']}

def reference(x, ctx_2048, fside_S_0, L0_xattn_W_q, L0_xattn_W_k, L0_xattn_W_v, L0_xattn_W_k_ip, L0_xattn_W_v_ip, L0_xattn_W_out, L0_xattn_b_out):
    import jax
    import jax.numpy as jnp

    def _L0_xattn_ref(hidden_states, encoder_hidden_states, spatial_mask, W_q, W_k, W_v, W_k_ip, W_v_ip, W_out, b_out):
        import jax, jax.numpy as jnp
        import numpy as np
        HEADS = 20
        NUM_TOKENS = 4
        IP_SCALE = 1.0
        SEM_SCALE = 0.5
        RESCALE = 1.0
        EPS = 1e-12

        def _l2norm(x, axis=-1):
            n = jnp.sqrt(jnp.sum(x * x, axis=axis, keepdims=True))
            return x / jnp.maximum(n, EPS)
        B, S, C = hidden_states.shape
        H = HEADS
        Dh = C // H
        attn_scale = Dh ** (-0.5)
        residual = hidden_states
        text_ehs = encoder_hidden_states[:, :-NUM_TOKENS]
        ip_ehs = encoder_hidden_states[:, -NUM_TOKENS:]

        def heads(x):
            return x.reshape(B, -1, H, Dh).transpose(0, 2, 1, 3)
        q = heads(hidden_states @ W_q)
        k_t = heads(text_ehs @ W_k)
        v_t = heads(text_ehs @ W_v)
        scores_t = jnp.einsum('bhsd,bhtd->bhst', q, k_t) * attn_scale
        probs_t = jax.nn.softmax(scores_t, axis=-1)
        text_out = jnp.einsum('bhst,bhtd->bhsd', probs_t, v_t)
        text_out = text_out.transpose(0, 2, 1, 3).reshape(B, S, C)
        k_ip = heads(ip_ehs @ W_k_ip)
        v_ip = heads(ip_ehs @ W_v_ip)
        attn_scores = jnp.einsum('bhsd,bhnd->bhsn', q, k_ip) * attn_scale
        qsem = jnp.einsum('bhst,bte->bhse', probs_t, text_ehs)
        qsem = _l2norm(qsem)
        ip_n = _l2norm(ip_ehs)
        sem = jnp.einsum('bhse,bne->bhsn', qsem, ip_n)
        sem = jax.lax.stop_gradient(sem)
        fused = attn_scores + SEM_SCALE * sem
        probs_ip = jax.nn.softmax(fused, axis=-1)
        probs_ip = probs_ip * spatial_mask[None, None, :, None]
        ip_out = jnp.einsum('bhsn,bhnd->bhsd', probs_ip, v_ip)
        ip_out = ip_out.transpose(0, 2, 1, 3).reshape(B, S, C)
        out = text_out + IP_SCALE * ip_out
        out = out @ W_out + b_out
        out = out + residual
        return out / RESCALE
    x = _L0_xattn_ref(x, ctx_2048, fside_S_0, L0_xattn_W_q, L0_xattn_W_k, L0_xattn_W_v, L0_xattn_W_k_ip, L0_xattn_W_v_ip, L0_xattn_W_out, L0_xattn_b_out)
    return x

_drawn_inputs = setup_inputs


def setup_inputs(seed=0):
    import zlib

    import numpy as np

    out = dict(_drawn_inputs(seed))
    spreads = {'L0_xattn_b_out': (0.0, 0.1)}
    factors = {}
    for name, (base, spread) in spreads.items():
        noise = np.random.default_rng([zlib.crc32(name.encode()), seed]).standard_normal(out[name].shape)
        drawn = base * np.exp(spread * noise) if base else spread * noise
        out[name] = jnp.asarray(drawn.astype(out[name].dtype))
    for name, factor in factors.items():
        out[name] = (out[name] * factor).astype(out[name].dtype)
    return out
```

```python
from contextlib import ExitStack

import concourse.bass as bass
from concourse import mybir

ALU = mybir.AluOpType
ACT = mybir.ActivationFunctionType
F16 = mybir.dt.float16
F32 = mybir.dt.float32
AX = mybir.AxisListType

P = 128
LN2 = 0.6931471805599453
EPS = 1e-12
SEM_SCALE = 0.5
X_SCALE = 64.0
K_SCALE = 32.0
HEADS = 20
IP = 4
DH = 8


def xattn(nc, x, xT, ctx, ctxT, smask, Wq, Wk, Wv, Wkip, Wvip, Wout, bout, ident, bdk_mask, bdv_mask, out):
    B, S, C = x.shape
    T = ctx.shape[1] - IP
    E = ctx.shape[2]
    NE = E // P
    NH = S // P
    BH = B * HEADS
    MG = 2
    CG = C // MG
    HG = HEADS // MG
    SOFT = DH ** -0.5
    Q_SCALE = 32.0 * SOFT
    S_SCALE = 2.0 ** -10
    P_SHIFT = 14 * LN2

    NT = (T + P - 1) // P
    TAIL = T - (NT - 1) * P
    G0 = (NT - 1) // 2 * P + TAIL
    GM = (T + 1) // 2
    MC = 400
    G1_FIRST = T - GM
    UNITS = (NT + 3) // 4
    KROWS = 3 * DH
    KR = KROWS + 2
    assert (NT - 1) % 4 == 0 and 2 * MC - 1 == GM and G0 >= GM and T - G0 == (NT - 1) // 2 * P

    def slot_token(slot):
        if slot == NT - 1:
            return (NT - 1) // 2 * P, TAIL
        u, k = divmod(slot, 4)
        return (2 * u + k, 0)[0] * P if k < 2 else G0 + (2 * u + k - 2) * P, P

    def slot_column(slot):
        t0, n = slot_token(slot)
        return (0, t0, n) if slot == NT - 1 or slot % 4 < 2 else (1, t0 - G1_FIRST, n)

    CG_IP = E
    CG_ONE = E + IP
    CG_V = CG_ONE + 1
    W_AUG = CG_V + DH
    W_RES = W_AUG - E

    k_dram = nc.dram_tensor("k_stacked", (BH, KROWS, T), F16).ap()
    q_dram = nc.dram_tensor("q_stacked", (BH, KROWS, S), F16).ap()

    with ExitStack() as st:
        def sb(name, shape, dt):
            return st.enter_context(nc.sbuf_tensor(name, shape, dt))

        def psum(name, shape, dt):
            return st.enter_context(nc.psum_tensor(name, shape, dt))

        def sem(name):
            return st.enter_context(nc.semaphore(name))

        ctx_parts = sb("ctx_parts", [P, B, 2, NT, CG_V], F16)
        v_parts = sb("v_parts", [P, 2, NT, B * C], F16)
        wout_sb = sb("wout_sb", [CG, MG, C], F32)
        bout_sb = sb("bout_sb", [1, C], F32)
        ones_sb = sb("ones_sb", [P, P], F32)
        ident32 = sb("ident32", [P, P], F32)
        ident16 = sb("ident16", [P, P], F16)
        smask_sb = sb("smask_sb", [P, NH], F32)
        x_sb = sb("x_sb", [P, B * NH, C], F32)
        ip_scores = sb("ip_scores", [P, B, HEADS, NH, IP], F32)
        ip_values = sb("ip_values", [HEADS * IP, B * C], F32)
        heads_out = sb("heads_out", [P, BH, NH, W_RES], F32)
        sem_sq = sb("sem_sq", [P, BH, NH], F32)
        half_pow = sb("half_pow", [P, HEADS * NH], F32)
        k_sb = sb("k_sb", [P, 2, G0], F16)
        q_sb = sb("q_sb", [P, 2, S], F16)
        q_max = sb("q_max", [P, S], F16)
        max_cols = sb("max_cols", [P, NH, P], F16)
        aug = sb("aug", [P, 2, 2, NT, W_AUG + W_AUG % 2], F16)
        p_hi = sb("p_hi", [P, 2, NT, S], F16)
        p_lo = sb("p_lo", [P, 2, NT, S], F16)
        p_32 = sb("p_32", [P, NT, S], F32)
        mx = sb("mx", [P, NH, 2], F32)
        mx1 = sb("mx1", [P, NH], F32)
        den = sb("den", [P, HEADS, NH], F32)
        eps_sq = sb("eps_sq", [P, HEADS, NH], F32)
        guard = sb("guard", [P, HEADS, NH], F32)
        rnorm = sb("rnorm", [P, HEADS, NH], F32)
        rden = sb("rden", [P, HEADS, NH], F32)
        fused = sb("fused", [P, HEADS, NH, IP], F32)
        fmax = sb("fmax", [P, HEADS, NH], F32)
        probs = sb("probs", [P, NH, HEADS, IP], F32)
        text = sb("text", [P, NH, C], F32)
        probsT = sb("probsT", [HEADS * IP, NH, P], F32)
        ip_values_b = sb("ip_values_b", [HEADS * IP, C], F32)
        fsum = sb("fsum", [P, HEADS, NH], F32)
        rsum = sb("rsum", [P, HEADS, NH], F32)
        oT = sb("oT", [CG, MG, S], F32)

        max_ps = psum("max_ps", [P, 2, 512], F32)
        sc_ps = [psum(f"sc_ps{i}", [P, 2, 512], F32) for i in range(2)]
        val_ps = [psum(f"val_ps{i}", [P, 512], F32) for i in range(2)]

        q_in = sem("q_in")
        w_in = sem("w_in")
        c_in = [sem(f"c_in{b}") for b in range(B)]
        cT_in = [sem(f"cT_in{b}") for b in range(B)]
        init = sem("init")
        pro_pe = sem("pro_pe")
        pro_act = sem("pro_act")
        pro_dve = sem("pro_dve")
        pro_pool = sem("pro_pool")
        q_out = sem("q_out")
        k_out = [sem(f"k_out{g}") for g in range(MG)]
        aug_in = [sem(f"aug_in{i}") for i in range(2)]
        kq_in = [sem(f"kq_in{i}") for i in range(2)]
        max_scores = sem("max_scores")
        max_free = sem("max_free")
        max_parts = sem("max_parts")
        max_one = sem("max_one")
        max_rows = sem("max_rows")
        scores = sem("scores")
        exps = sem("exps")
        lo_dve = sem("lo_dve")
        lo_pool = sem("lo_pool")
        v_cols = sem("v_cols")
        val_done = [sem(f"val_done{i}") for i in range(NH)]
        val_read = [sem(f"val_read{i}") for i in range(NH)]
        post_dve = sem("post_dve")
        post_act = sem("post_act")
        post_pool = sem("post_pool")
        post_pe = sem("post_pe")
        y_out = sem("y_out")

        def view(tensor, start, shape, dt):
            flat = tensor[0:shape[0]]
            size = shape[1] * shape[2] * (2 if dt == F32 else 1)
            flat = flat.rearrange("p a b c -> p (a b c)") if len(flat.shape) == 4 else flat.rearrange("p a b c d -> p (a b c d)")
            part = flat[:, start:start + size]
            part = part.bitcast(F32) if dt == F32 else part
            return part.rearrange("p (a b) -> p a b", a=shape[1])

        TALL = T + IP
        c_rows = p_32
        cT = [view(p_hi, 0, [P, NE, TALL], F32), view(p_lo, 0, [P, NE, TALL], F32)]
        kh = view(aug, 0, [CG, MG, TALL], F16)
        kl = view(aug, MG * TALL, [CG, MG, TALL], F16)
        at = 2 * MG * TALL
        qh = view(aug, at, [CG, MG, B * S], F16)
        xT_sb = view(aug, at + MG * B * S, [CG, MG, B * S], F32)
        wq_sb = view(aug, at + 3 * MG * B * S, [CG, MG, C], F32)
        ql = sb("ql", [CG, MG, B * S], F16)
        qT_sb = sb("qT_sb", [CG, MG, B * S], F32)
        wk_sb = sb("wk_sb", [P, NE, C], F32)
        wv_sb = sb("wv_sb", [P, 2, NE, C + IP], F32)
        wip = heads_out[:].rearrange("p a b c -> p (a b c)")[:, 0:2 * NE * C].rearrange("p (w e c) -> p w e c", w=2, e=NE)
        wkip_sb, wvip_sb = wip[:, 0], wip[:, 1]
        bdk_mask_sb = sb("bdk_mask_sb", [CG, HG], F32)
        bdv_mask_sb = sb("bdv_mask_sb", [HEADS * IP, C], F32)
        ip_sq = sb("ip_sq", [P, NE, IP], F32)
        ip_rep = sb("ip_rep", [P, NE, HEADS, IP], F32)
        ip_n2 = sb("ip_n2", [P, IP], F32)
        ip_rn = sb("ip_rn", [P, IP], F32)
        kipT = sb("kipT", [CG, MG, IP], F32)
        bdk = sb("bdk", [CG, MG, HG, IP], F32)

        block = st.enter_context(nc.Block())

        N_WIN = 11

        V_PER = 3
        V_USES = (NT + V_PER - 1) // V_PER
        K_USES = 2 * MG

        def tally(order):
            return {name: i + 1 for i, name in enumerate(order)}

        V_ALL = [("v", i) for i in range(V_USES)]
        PE_AT = tally([("q", mg) for mg in range(MG)] + [(b,) + w for b in range(B) for w in [
            ("n2",), ("k", 0), ("kv",), ("k", 1), ("ips",), ("k", 2), ("k", 3)] + V_ALL])
        ACT_AT = tally([("q", mg) for mg in range(MG)] + [(b,) + w for b in range(B) for w in [
            ("k", 0), ("k", 1), ("ips",), ("k", 2), ("k", 3), ("x",)] + V_ALL])
        DVE_AT = tally(["init"] + [("q", mg) for mg in range(MG)] + [(b,) + w for b in range(B) for w in [
            ("rep",), ("n2",), ("k", 0), ("kv",), ("bdk",), ("k", 1), ("unit",), ("k", 2), ("k", 3), ("x",)] + V_ALL])
        POOL_AT = tally(["init"] + [(b, "rn") for b in range(B)])
        V_END = ("v", V_USES - 1)

        def v_use(i):
            s0 = V_PER * i
            k = min(V_PER, NT - s0)
            rows = P if s0 + k < NT else TAIL
            assert rows == P or k == 1
            bank = [val_ps[0][:, :], val_ps[1][:, :], max_ps[:, 0, :], max_ps[:, 1, :]][i % 4]
            return s0, k, rows, bank[0:rows, 0:k * (C + IP)].rearrange("p (s c) -> p s c", s=k)

        POST_AT = tally(["den", "eps", "guard", "rden", "dots", "fused", "fmax", "shifted", "fsum", "rsum", "masked",
                         "probs", "text", "probsT", "oT", "y"])
        POST_DVE = len(POST_AT)

        def unit_slots(u):
            return (4 * u, min(4, NT - 4 * u), P if u < UNITS - 1 else TAIL)

        def lo_unit(engine, u, par):
            s0, k, rows = unit_slots(u)
            return engine.tensor_tensor(p_lo[0:rows, par, s0:s0 + k, :], p_32[0:rows, s0:s0 + k, :],
                                        p_hi[0:rows, par, s0:s0 + k, :], ALU.subtract)


        @block.sync
        def _(sp):
            def head_load(n, par):
                for g in range(2):
                    cols = slice(0, G0) if g == 0 else slice(G1_FIRST, T)
                    w = G0 if g == 0 else GM
                    sp.dma_start(k_sb[64 * g:64 * g + KROWS, par, 0:w],
                                 k_dram[bass.ds(n, 1), :, cols].rearrange("o r t -> (o r) t")).then_inc(kq_in[par], 16)
                    sp.dma_start(q_sb[64 * g:64 * g + KROWS, par, :],
                                 q_dram[bass.ds(n, 1), :, :].rearrange("o r t -> (o r) t")).then_inc(kq_in[par], 16)

            def aug_load(b, par):
                sp.dma_start(aug[:, par, :, :, 0:CG_V].rearrange("p w s c -> p (w s) c"),
                             ctx_parts[:, bass.ds(b, 1), :, :, :].rearrange("p o w s c -> p (o w s) c")
                             ).then_inc(aug_in[par], 16)

            sp.dma_start(xT_sb, xT.rearrange("(g c) t -> c g t", g=MG)).then_inc(q_in, 16)
            sp.dma_start(wq_sb, Wq.rearrange("(g c) n -> c g n", g=MG)).then_inc(q_in, 16)
            sp.dma_start(ident32[:], ident).then_inc(q_in, 16)

            def rows_load(b):
                for s in range(NT):
                    t0, n = slot_token(s)
                    sp.dma_start(c_rows[0:n, s, :], ctx[b, t0:t0 + n, :]).then_inc(c_in[b], 16)

            def columns_load(b):
                sp.dma_start(cT[b % 2], ctxT[b].rearrange("(e p) t -> p e t", p=P)).then_inc(cT_in[b], 16)

            columns_load(0)
            rows_load(0)
            columns_load(1)
            for b in range(B):
                for mg in range(MG):
                    sp.wait_ge(pro_dve, DVE_AT[b, "k", 2 * mg + 1])
                    for r, part in enumerate([kh, kl, kh]):
                        sp.dma_start(k_dram[b * HEADS + mg * HG:b * HEADS + (mg + 1) * HG, r * DH:(r + 1) * DH, :],
                                     part[:, mg, 0:T]).then_inc(k_out[mg], 16)
                if b + 1 < B:
                    sp.wait_ge(pro_dve, DVE_AT[b, "x"])
                    rows_load(b + 1)
                if b + 2 < B:
                    sp.wait_ge(pro_pe, PE_AT[(b,) + V_END])
                    sp.wait_ge(pro_dve, DVE_AT[b, "unit"])
                    columns_load(b + 2)
            for mg in range(MG):
                sp.wait_ge(k_out[mg], 16 * 3 * B)
            sp.wait_ge(q_out, 16 * 3 * MG * B)
            sp.wait_ge(pro_pool, POOL_AT["init"])
            head_load(0, 0)
            head_load(1, 1)
            sp.wait_ge(pro_dve, DVE_AT[(0,) + V_END])
            aug_load(0, 0)
            aug_load(0, 1)
            sp.wait_ge(scores, UNITS)
            head_load(2, 0)

            def step(n, par):
                sp.wait_ge(scores, UNITS * (n + 2))
                head_load(n + 3, 1 - par)

            def aug_step(b):
                sp.wait_ge(val_done[1], b * HEADS - 1)
                aug_load(b, 0)
                sp.wait_ge(val_done[1], b * HEADS)
                aug_load(b, 1)

            def store(b):
                sp.wait_ge(post_dve, POST_DVE * (b + 1))
                sp.dma_start(out[bass.ds(b, 1), :, :].rearrange("o (h p) c -> p (o h) c", p=P),
                             x_sb[:, bass.ds(b * NH, NH), :]).then_inc(y_out, 16)

            step(0, 0)
            step(1, 1)
            with sp.Fori(0, B - 1) as b:
                with sp.Fori(0, HEADS // 2 - 1) as j:
                    n = b * HEADS + j * 2 + 2
                    step(n, 0)
                    step(n + 1, 1)
                n = b * HEADS + HEADS
                aug_step(b + 1)
                step(n, 0)
                step(n + 1, 1)
                store(b)
            with sp.Fori(0, HEADS // 2 - 3) as j:
                n = j * 2 + ((B - 1) * HEADS + 2)
                step(n, 0)
                step(n + 1, 1)
            step(BH - 4, 0)
            store(B - 1)
            sp.wait_ge(y_out, 16 * B)

        @block.gpsimd
        def _(pool):
            nc.gpsimd.memset(k_sb[:], -K_SCALE * 32.0)
            nc.gpsimd.memset(ctx_parts[:, :, :, NT - 1, 0:CG_ONE], 0.0)
            nc.gpsimd.memset(v_parts[:, :, NT - 1, :], 0.0)
            nc.gpsimd.memset(q_sb[:], 0.0)
            nc.gpsimd.memset(max_cols[:], 0.0)
            nc.gpsimd.memset(half_pow[:], -0.5)
            nc.gpsimd.memset(ctx_parts[:, :, 0, :, CG_ONE:CG_V], X_SCALE)
            nc.gpsimd.memset(ctx_parts[:, :, 1, :, CG_ONE:CG_V], 0.0).then_inc(pro_pool, 1)
            for b in range(B):
                pool.wait_ge(pro_dve, DVE_AT[b, "n2"])
                if b == 0:
                    pool.wait_ge(pro_pool, POOL_AT["init"])
                nc.gpsimd.tensor_tensor(ip_rn[:], ip_n2[:], half_pow[:, 0:IP], ALU.pow).then_inc(pro_pool, 1)

            def values_of(m, par):
                nc.gpsimd.tensor_copy(aug[:, par, :, :, CG_V:W_AUG],
                                      v_parts[:, :, :, bass.ds(m * DH, DH)]).then_inc(v_cols, 1)

            def lo_parts(m, par):
                for u in (1, 3):
                    pool.wait_ge(exps, UNITS * m + (u + 1))
                    lo_unit(nc.gpsimd, u, par).then_inc(lo_pool, 1)

            def head(m, par, b):
                pool.wait_ge(val_done[1], m - 1)
                pool.wait_ge(aug_in[par], 16 * (b + 1))
                values_of(m, par)
                lo_parts(m, par)

            def post(b):
                pool.wait_ge(post_dve, POST_DVE * b + POST_AT["guard"])
                nc.gpsimd.tensor_tensor(rnorm[:].rearrange("p h n -> p (h n)"), guard[:].rearrange("p h n -> p (h n)"),
                                        half_pow[:], ALU.pow).then_inc(post_pool, 1)
                nc.gpsimd.tensor_copy(ip_values_b[:], ip_values[:, bass.ds(b * C, C)]).then_inc(post_pool, 1)

            pool.wait_ge(pro_dve, DVE_AT[(B - 1,) + V_END])
            for m in range(2):
                pool.wait_ge(aug_in[m], 16)
                values_of(m, m)
                lo_parts(m, m)
            with pool.Fori(0, B - 1) as b:
                with pool.Fori(0, HEADS // 2 - 1) as j:
                    m = b * HEADS + j * 2 + 2
                    head(m, 0, b)
                    head(m + 1, 1, b)
                m = b * HEADS + HEADS
                head(m, 0, b + 1)
                post(b)
                head(m + 1, 1, b + 1)
            with pool.Fori(0, HEADS // 2 - 1) as j:
                m = j * 2 + ((B - 1) * HEADS + 2)
                head(m, 0, B - 1)
                head(m + 1, 1, B - 1)
            post(B - 1)

        @block.scalar
        def _(act):
            act.dma_start(wk_sb[:], Wk.rearrange("(e p) n -> p e n", p=P)).then_inc(w_in, 16)
            act.dma_start(wkip_sb, Wkip.rearrange("(e p) n -> p e n", p=P)).then_inc(w_in, 16)
            act.dma_start(wvip_sb, Wvip.rearrange("(e p) n -> p e n", p=P)).then_inc(w_in, 16)
            for i in range(2):
                act.dma_start(wv_sb[:, i, :, 0:C], Wv.rearrange("(e p) n -> p e n", p=P)).then_inc(w_in, 16)
            act.dma_start(bdk_mask_sb[:], bdk_mask).then_inc(w_in, 16)
            act.dma_start(bdv_mask_sb[:], bdv_mask).then_inc(w_in, 16)
            act.dma_start(wout_sb[:], Wout.rearrange("(g c) n -> c g n", g=MG)).then_inc(w_in, 16)
            act.dma_start(bout_sb[:], bout.rearrange("(o c) -> o c", o=1)).then_inc(w_in, 16)
            act.dma_start(smask_sb[:], smask).then_inc(w_in, 16)
            act.dma_start(x_sb[:], x.rearrange("b (h p) c -> p (b h) c", p=P)).then_inc(w_in, 16)

            act.wait_ge(pro_pool, POOL_AT["init"])
            for mg in range(MG):
                act.wait_ge(pro_pe, PE_AT["q", mg])
                src = sc_ps[mg][0:CG, :, :].rearrange("c a t -> c (a t)")
                nc.scalar.activation(qT_sb[:, mg, :], src, ACT.Copy)
                nc.scalar.activation(qh[:, mg, :], src, ACT.Copy, scale=Q_SCALE).then_inc(pro_act, 1)
            for mg in range(MG):
                act.wait_ge(pro_dve, DVE_AT["q", mg])
                for r, part in enumerate([qh, qh, ql]):
                    for b in range(B):
                        act.dma_start(q_dram[b * HEADS + mg * HG:b * HEADS + (mg + 1) * HG, r * DH:(r + 1) * DH, :],
                                      part[:, mg, b * S:(b + 1) * S]).then_inc(q_out, 16)

            def key_hi(b, i):
                mg, c = divmod(i, 2)
                act.wait_ge(pro_pe, PE_AT[b, "k", i])
                if b >= 1 and c == 0:
                    act.wait_ge(k_out[mg], 16 * 3 * b)
                nc.scalar.activation(kh[:, mg, 2 * MC * c:2 * MC * (c + 1)].rearrange("p (a t) -> p a t", a=2),
                                     sc_ps[c][0:CG, :, 0:MC], ACT.Copy, scale=K_SCALE).then_inc(pro_act, 1)

            for b in range(B):
                key_hi(b, 0)
                key_hi(b, 1)
                act.wait_ge(pro_pe, PE_AT[b, "ips"])
                nc.scalar.activation(ip_scores[:, b, :, :, :],
                                     max_ps[:, 0, 0:NH * HEADS * IP].rearrange("p (a h i) -> p h a i", a=NH, h=HEADS),
                                     ACT.Copy, scale=SOFT).then_inc(pro_act, 1)
                key_hi(b, 2)
                key_hi(b, 3)
                act.wait_ge(c_in[b], 16 * NT)
                nc.scalar.activation(ctx_parts[:, b, 0, 0:NT - 1, 0:E], c_rows[:, 0:NT - 1, :], ACT.Copy, scale=X_SCALE)
                nc.scalar.activation(ctx_parts[0:TAIL, b, 0, NT - 1, 0:E], c_rows[0:TAIL, NT - 1, :], ACT.Copy,
                                     scale=X_SCALE).then_inc(pro_act, 1)
                for i in range(V_USES):
                    s0, k, rows, src = v_use(i)
                    act.wait_ge(pro_pe, PE_AT[b, "v", i])
                    nc.scalar.activation(v_parts[0:rows, 0, s0:s0 + k, b * C:(b + 1) * C], src[:, :, 0:C], ACT.Copy,
                                         scale=X_SCALE)
                    nc.scalar.activation(ctx_parts[0:rows, b, 0, s0:s0 + k, CG_IP:CG_ONE], src[:, :, C:C + IP],
                                         ACT.Copy, scale=X_SCALE).then_inc(pro_act, 1)

            def exp_unit(m, u, par, first=False):
                act.wait_ge(scores, UNITS * m + (u + 1))
                if not first:
                    if u % 2 == 0:
                        act.wait_ge(lo_dve, 2 * m - 2 + (u // 2 + 1))
                    else:
                        act.wait_ge(lo_pool, 2 * m - 2 + (u // 2 + 1))
                s0, k, rows = unit_slots(u)
                src = sc_ps[u % 2][0:rows, :, :].rearrange("p a t -> p (a t)")[:, 0:k * S]
                nc.scalar.activation(p_32[0:rows, s0:s0 + k, :].rearrange("p s q -> p (s q)"), src, ACT.Exp,
                                     bias=P_SHIFT, scale=S_SCALE)
                nc.scalar.activation(p_hi[0:rows, par, s0:s0 + k, :].rearrange("p s q -> p (s q)"), src, ACT.Exp,
                                     bias=P_SHIFT, scale=S_SCALE).then_inc(exps, 1)

            def read_values(n, half):
                act.wait_ge(val_done[half], n + 1)
                nc.scalar.activation(val_ps[half][:, 0:E], val_ps[half][:, 0:E], ACT.Square,
                                     accum_out=sem_sq[:, bass.ds(n, 1), half])
                nc.scalar.activation(heads_out[:, bass.ds(n, 1), half, :].rearrange("p o c -> p (o c)"),
                                     val_ps[half][:, E:W_AUG], ACT.Copy).then_inc(val_read[half], 1)

            def post_exp(b):
                act.wait_ge(post_dve, POST_DVE * b + POST_AT["shifted"])
                nc.scalar.activation(fused[:].rearrange("p h n i -> p (h n i)"),
                                     fused[:].rearrange("p h n i -> p (h n i)"), ACT.Exp).then_inc(post_act, 1)

            def step(n, par, has_next=True, post_b=None):
                if has_next:
                    act.wait_ge(val_done[1], n)
                    exp_unit(n + 1, 0, 1 - par)
                    exp_unit(n + 1, 1, 1 - par)
                    exp_unit(n + 1, 2, 1 - par)
                if post_b is not None:
                    post_exp(post_b)
                read_values(n, 0)
                if has_next:
                    exp_unit(n + 1, 3, 1 - par)
                read_values(n, 1)

            act.wait_ge(pro_dve, DVE_AT[(B - 1,) + V_END])
            for u in range(UNITS):
                exp_unit(0, u, 0, first=True)
            step(0, 0)
            step(1, 1)
            with act.Fori(0, B - 1) as b:
                with act.Fori(0, HEADS // 2 - 1) as j:
                    n = b * HEADS + j * 2 + 2
                    step(n, 0)
                    step(n + 1, 1)
                n = b * HEADS + HEADS
                step(n, 0, post_b=b)
                step(n + 1, 1)
            with act.Fori(0, HEADS // 2 - 2) as j:
                n = j * 2 + ((B - 1) * HEADS + 2)
                step(n, 0)
                step(n + 1, 1)
            step(BH - 2, 0)
            step(BH - 1, 1, has_next=False)
            post_exp(B - 1)

        @block.vector
        def _(dve):
            done = [0]

            def step_done(instruction, name):
                done[0] += 1
                assert DVE_AT[name] == done[0], name
                instruction.then_inc(pro_dve, 1)

            dve.wait_ge(q_in, 48)
            nc.vector.tensor_copy(ident16[:], ident32[:])
            step_done(nc.vector.memset(ones_sb[:], 1.0), "init")
            for mg in range(MG):
                dve.wait_ge(pro_act, ACT_AT["q", mg])
                step_done(nc.vector.scalar_tensor_tensor(
                    out=ql[:, mg, :], in0=sc_ps[mg][0:CG, :, :].rearrange("c a t -> c (a t)"), scalar=Q_SCALE,
                    in1=qh[:, mg, :], op0=ALU.mult, op1=ALU.subtract), ("q", mg))
            dve.wait_ge(w_in, 16 * N_WIN)

            def key_lo(b, i):
                mg, c = divmod(i, 2)
                dve.wait_ge(pro_act, ACT_AT[b, "k", i])
                cols = slice(2 * MC * c, 2 * MC * (c + 1))
                step_done(nc.vector.scalar_tensor_tensor(
                    out=kl[:, mg, cols].rearrange("p (a t) -> p a t", a=2), in0=sc_ps[c][0:CG, :, 0:MC],
                    scalar=K_SCALE, in1=kh[:, mg, cols].rearrange("p (a t) -> p a t", a=2),
                    op0=ALU.mult, op1=ALU.subtract), (b, "k", i))

            for b in range(B):
                ipT = cT[b % 2][:, :, T:TALL]
                dve.wait_ge(cT_in[b], 16)
                if b >= 1:
                    dve.wait_ge(pro_pe, PE_AT[b - 1, "kv"])
                nc.vector.tensor_copy(ip_rep[:], ipT.unsqueeze(2).to_broadcast([P, NE, HEADS, IP]))
                step_done(nc.vector.tensor_tensor(ip_sq[:], ipT, ipT, ALU.mult), (b, "rep"))
                dve.wait_ge(pro_pe, PE_AT[b, "n2"])
                step_done(nc.vector.tensor_scalar(ip_n2[:], max_ps[:, 0, 0:IP], EPS * EPS, None, ALU.max), (b, "n2"))
                key_lo(b, 0)
                dve.wait_ge(pro_pe, PE_AT[b, "kv"])
                nc.vector.tensor_copy(kipT[:], max_ps[0:CG, 1, 0:MG * IP].rearrange("p (g i) -> p g i", g=MG))
                step_done(nc.vector.tensor_tensor(ip_values[:, b * C:(b + 1) * C], max_ps[0:HEADS * IP, 1, 64:64 + C],
                                                  bdv_mask_sb[:], ALU.mult), (b, "kv"))
                dve.wait_ge(pro_dve, DVE_AT[b, "kv"])
                if b >= 1:
                    dve.wait_ge(pro_pe, PE_AT[b - 1, "ips"])
                for g in range(MG):
                    last = nc.vector.tensor_tensor(bdk[:, g, :, :],
                                                   kipT[:, g, :].unsqueeze(1).to_broadcast([CG, HG, IP]),
                                                   bdk_mask_sb[:].unsqueeze(2).to_broadcast([CG, HG, IP]), ALU.mult)
                step_done(last, (b, "bdk"))
                key_lo(b, 1)
                dve.wait_ge(pro_pool, POOL_AT[b, "rn"])
                step_done(nc.vector.tensor_tensor(wv_sb[:, b % 2, :, C:C + IP], ipT,
                                                  ip_rn[:].unsqueeze(1).to_broadcast([P, NE, IP]), ALU.mult),
                          (b, "unit"))
                key_lo(b, 2)
                key_lo(b, 3)
                dve.wait_ge(pro_act, ACT_AT[b, "x"])
                for rows, slots in ((P, slice(0, NT - 1)), (TAIL, slice(NT - 1, NT))):
                    last = nc.vector.scalar_tensor_tensor(
                        out=ctx_parts[0:rows, b, 1, slots, 0:E], in0=c_rows[0:rows, slots, :], scalar=X_SCALE,
                        in1=ctx_parts[0:rows, b, 0, slots, 0:E], op0=ALU.mult, op1=ALU.subtract)
                step_done(last, (b, "x"))
                for i in range(V_USES):
                    s0, k, rows, src = v_use(i)
                    dve.wait_ge(pro_act, ACT_AT[b, "v", i])
                    nc.vector.scalar_tensor_tensor(
                        out=v_parts[0:rows, 1, s0:s0 + k, b * C:(b + 1) * C], in0=src[:, :, 0:C], scalar=X_SCALE,
                        in1=v_parts[0:rows, 0, s0:s0 + k, b * C:(b + 1) * C], op0=ALU.mult, op1=ALU.subtract)
                    step_done(nc.vector.scalar_tensor_tensor(
                        out=ctx_parts[0:rows, b, 1, s0:s0 + k, CG_IP:CG_ONE], in0=src[:, :, C:C + IP], scalar=X_SCALE,
                        in1=ctx_parts[0:rows, b, 0, s0:s0 + k, CG_IP:CG_ONE], op0=ALU.mult, op1=ALU.subtract),
                        (b, "v", i))

            def chunk_max(m, c):
                dve.wait_ge(max_scores, 4 * m + (c + 1))
                nc.vector.tensor_reduce(mx[:, c // 2, c % 2:c % 2 + 1], max_ps[:, :, 0:MC], AX.XY,
                                        ALU.max).then_inc(max_free, 1)

            part_cols = max_cols[:].rearrange("p n (g c) -> p n g c", g=2)

            def max_to_rows(m, par, first=False):
                dve.wait_ge(max_free, 5 * m + 4)
                nc.vector.tensor_tensor(mx1[:], mx[:, :, 0], mx[:, :, 1], ALU.max).then_inc(max_one, 1)
                dve.wait_ge(max_one, m + 1)
                nc.vector.tensor_scalar(part_cols[:, :, :, KROWS], mx1[:].unsqueeze(2).to_broadcast([P, NH, 2]),
                                        S_SCALE, None, ALU.mult).then_inc(max_parts, 1)
                dve.wait_ge(max_parts, 2 * m + 1)
                nc.vector.scalar_tensor_tensor(out=part_cols[:, :, :, KROWS + 1],
                                               in0=mx1[:].unsqueeze(2).to_broadcast([P, NH, 2]), scalar=S_SCALE,
                                               in1=part_cols[:, :, :, KROWS], op0=ALU.mult,
                                               op1=ALU.subtract).then_inc(max_parts, 1)
                dve.wait_ge(max_rows, m + 1)
                if not first:
                    dve.wait_ge(scores, UNITS * m)
                nc.vector.tensor_tensor(q_max[:], q_sb[:, par, :], max_ps[:, 0, 0:S], ALU.add).then_inc(max_free, 1)

            def lo_parts(m, u, par):
                dve.wait_ge(exps, UNITS * m + (u + 1))
                lo_unit(nc.vector, u, par).then_inc(lo_dve, 1)

            def post_step(b, name, instruction):
                instruction.then_inc(post_dve, 1)
                dve.wait_ge(post_dve, POST_DVE * b + POST_AT[name])

            def flat(t):
                return t[:].rearrange("p h n -> p (h n)")

            def columns(b, lo, hi):
                return heads_out[:, bass.ds(b * HEADS, HEADS), :, lo:hi].rearrange("p h n c -> p (h n) c")

            def post_norms(b):
                dve.wait_ge(val_read[1], (b + 1) * HEADS)
                post_step(b, "den", nc.vector.tensor_scalar(
                    flat(den), columns(b, IP, IP + 1).rearrange("p g c -> p (g c)"), 1.0, None, ALU.mult))
                ones = flat(den)
                post_step(b, "eps", nc.vector.scalar_tensor_tensor(out=flat(eps_sq), in0=ones, scalar=EPS * EPS,
                                                                   in1=ones, op0=ALU.mult, op1=ALU.mult))
                post_step(b, "guard", nc.vector.tensor_tensor(
                    flat(guard), flat(eps_sq), sem_sq[:, bass.ds(b * HEADS, HEADS), :].rearrange("p h n -> p (h n)"),
                    ALU.max))
                post_step(b, "rden", nc.vector.reciprocal(flat(rden), ones))

            fused_g = fused[:].rearrange("p h n i -> p (h n) i")
            GR = HEADS * NH

            def post_fused(b):
                dve.wait_ge(post_pool, 2 * b + 1)
                post_step(b, "dots", nc.vector.tensor_tensor(fused_g, columns(b, 0, IP),
                                                             flat(rnorm).unsqueeze(2).to_broadcast([P, GR, IP]),
                                                             ALU.mult))
                post_step(b, "fused", nc.vector.scalar_tensor_tensor(
                    out=fused[:].rearrange("p h n i -> p (h n i)"), in0=fused[:].rearrange("p h n i -> p (h n i)"),
                    scalar=SEM_SCALE, in1=ip_scores[:, bass.ds(b, 1), :, :, :].rearrange("p o h n i -> p (o h n i)"),
                    op0=ALU.mult, op1=ALU.add))
                post_step(b, "fmax", nc.vector.tensor_reduce(flat(fmax), fused_g, AX.X, ALU.max))
                post_step(b, "shifted", nc.vector.tensor_tensor(fused_g, fused_g,
                                                                flat(fmax).unsqueeze(2).to_broadcast([P, GR, IP]),
                                                                ALU.subtract))

            def post_probs(b):
                dve.wait_ge(post_act, b + 1)
                post_step(b, "fsum", nc.vector.tensor_reduce(flat(fsum), fused_g, AX.X, ALU.add))
                post_step(b, "rsum", nc.vector.reciprocal(flat(rsum), flat(fsum)))
                post_step(b, "masked", nc.vector.tensor_tensor(rsum[:], rsum[:],
                                                               smask_sb[:].unsqueeze(1).to_broadcast([P, HEADS, NH]),
                                                               ALU.mult))
                post_step(b, "probs", nc.vector.tensor_tensor(probs[:].rearrange("p n h i -> p h n i"), fused[:],
                                                              rsum[:].unsqueeze(3).to_broadcast([P, HEADS, NH, IP]),
                                                              ALU.mult))
                post_step(b, "text", nc.vector.tensor_tensor(
                    text[:].rearrange("p n (h d) -> p h n d", d=DH),
                    heads_out[:, bass.ds(b * HEADS, HEADS), :, IP + 1:W_RES],
                    rden[:].unsqueeze(3).to_broadcast([P, HEADS, NH, DH]), ALU.mult))

            def post_copy(b, k, name, out_, in_):
                dve.wait_ge(post_pe, 3 * b + k)
                post_step(b, name, nc.vector.tensor_copy(out_, in_))

            def post_probsT(b):
                post_copy(b, 1, "probsT", probsT[:].rearrange("p n s -> p (n s)"), max_ps[0:HEADS * IP, 0, 0:S])

            def post_oT(b):
                post_copy(b, 2, "oT", oT[:].rearrange("p g s -> p (g s)"), max_ps[0:CG, 0, 0:MG * S])

            def post_y(b):
                x_rows = x_sb[:, bass.ds(b * NH, NH), :].rearrange("p n c -> p (n c)")
                dve.wait_ge(post_pe, 3 * b + 3)
                post_step(b, "y", nc.vector.tensor_tensor(
                    x_rows, max_ps[:, 0, 0:NH * C], x_rows, ALU.add))

            def step(n, par, maxima=True, post=None):
                post = post or {}
                if maxima:
                    chunk_max(n + 2, 0)
                post.get(0, lambda: None)()
                lo_parts(n + 1, 0, 1 - par)
                if maxima:
                    chunk_max(n + 2, 1)
                post.get(1, lambda: None)()
                if maxima:
                    chunk_max(n + 2, 2)
                lo_parts(n + 1, 2, 1 - par)
                post.get(2, lambda: None)()
                if maxima:
                    chunk_max(n + 2, 3)
                    max_to_rows(n + 2, par)
                post.get(3, lambda: None)()

            for m in range(2):
                for c in range(4):
                    chunk_max(m, c)
                if m == 0:
                    dve.wait_ge(pro_pool, POOL_AT["init"])
                    dve.wait_ge(kq_in[0], 64)
                max_to_rows(m, m, first=(m == 0))
            lo_parts(0, 0, 0)
            lo_parts(0, 2, 0)
            step(0, 0)
            step(1, 1)
            with dve.Fori(0, B - 1) as b:
                with dve.Fori(0, HEADS // 2 - 1) as j:
                    n = b * HEADS + j * 2 + 2
                    step(n, 0)
                    step(n + 1, 1)
                n = b * HEADS + HEADS
                step(n, 0, post={0: lambda: post_norms(b), 1: lambda: post_fused(b), 2: lambda: post_probs(b),
                                 3: lambda: post_probsT(b)})
                step(n + 1, 1, post={0: lambda: post_oT(b), 1: lambda: post_y(b)})
            with dve.Fori(0, HEADS // 2 - 2) as j:
                n = j * 2 + ((B - 1) * HEADS + 2)
                step(n, 0)
                step(n + 1, 1)
            step(BH - 2, 0, maxima=False)
            for stage in (post_norms, post_fused, post_probs, post_probsT, post_oT, post_y):
                stage(B - 1)

        @block.tensor
        def _(pe):
            done = [0]

            def step_done(instruction, name):
                done[0] += 1
                assert PE_AT[name] == done[0], name
                instruction.then_inc(pro_pe, 1)

            pe.wait_ge(q_in, 48)
            for mg in range(MG):
                for a in range(2):
                    for g in range(MG):
                        last = nc.tensor.matmul(sc_ps[mg][0:CG, a, :], wq_sb[:, g, mg * CG:(mg + 1) * CG],
                                                xT_sb[:, g, a * 512:(a + 1) * 512], start=(g == 0), stop=(g == MG - 1))
                step_done(last, ("q", mg))

            def keys(b, i):
                mg, c = divmod(i, 2)
                pe.wait_ge(pro_dve, DVE_AT[b, "k", i - 2] if i >= 2 else DVE_AT[b - 1, "k", i + 2] if b else DVE_AT["q", c])
                for a in range(2):
                    cols = slice((2 * c + a) * MC, (2 * c + a + 1) * MC)
                    for e in range(NE):
                        last = nc.tensor.matmul(sc_ps[c][0:CG, a, 0:MC], wk_sb[:, e, mg * CG:(mg + 1) * CG],
                                                cT[b % 2][:, e, cols], start=(e == 0), stop=(e == NE - 1))
                step_done(last, (b, "k", i))

            pe.wait_ge(w_in, 16 * N_WIN)
            for b in range(B):
                ipT = cT[b % 2][:, :, T:TALL]
                pe.wait_ge(cT_in[b], 16)
                pe.wait_ge(pro_dve, DVE_AT[b, "rep"])
                for e in range(NE):
                    last = nc.tensor.matmul(max_ps[:, 0, 0:IP], ones_sb[:], ip_sq[:, e, :], start=(e == 0), stop=(e == NE - 1))
                step_done(last, (b, "n2"))
                keys(b, 0)
                for mg in range(MG):
                    for e in range(NE):
                        nc.tensor.matmul(max_ps[0:CG, 1, mg * IP:(mg + 1) * IP], wkip_sb[:, e, mg * CG:(mg + 1) * CG],
                                         ipT[:, e, :], start=(e == 0), stop=(e == NE - 1))
                for e in range(NE):
                    last = nc.tensor.matmul(max_ps[0:HEADS * IP, 1, 64:64 + C],
                                            ip_rep[:, e, :, :].rearrange("p h i -> p (h i)"), wvip_sb[:, e, :],
                                            start=(e == 0), stop=(e == NE - 1))
                step_done(last, (b, "kv"))
                keys(b, 1)
                pe.wait_ge(pro_dve, DVE_AT[b, "bdk"])
                for half in range(NH):
                    for mg in range(MG):
                        q0 = b * S + half * P
                        c0 = (half * MG + mg) * HG * IP
                        last = nc.tensor.matmul(max_ps[:, 0, c0:c0 + HG * IP], qT_sb[:, mg, q0:q0 + P],
                                                bdk[:, mg, :, :].rearrange("p h i -> p (h i)"), start=True, stop=True)
                step_done(last, (b, "ips"))
                keys(b, 2)
                keys(b, 3)
                pe.wait_ge(pro_dve, DVE_AT[b, "unit"])
                for i in range(V_USES):
                    if i == 2:
                        pe.wait_ge(pro_act, ACT_AT[b, "ips"])
                    if i == 4:
                        pe.wait_ge(pro_dve, DVE_AT[b, "v", 0])
                    s0, k, rows, dst = v_use(i)
                    for s in range(s0, s0 + k):
                        t0, n = slot_token(s)
                        for e in range(NE):
                            last = nc.tensor.matmul(dst[:, s - s0, :], cT[b % 2][:, e, t0:t0 + n],
                                                    wv_sb[:, b % 2, e, :], start=(e == 0), stop=(e == NE - 1))
                    step_done(last, (b, "v", i))
                pe.wait_ge(pro_dve, DVE_AT[(b,) + V_END])

            def max_chunk(m, g, c, par):
                half, chunk = divmod(c, 2)
                if c == 0:
                    pe.wait_ge(kq_in[par], 64 * (g + 1))
                pe.wait_ge(max_free, 5 * m + c)
                col = chunk * (MC - 1)
                for r in range(2):
                    last = nc.tensor.matmul(max_ps[:, r, 0:MC], q_sb[64 * r:64 * r + KR, par, half * P:(half + 1) * P],
                                            k_sb[64 * r:64 * r + KR, par, col:col + MC], start=True, stop=True)
                last.then_inc(max_scores, 1)

            def max_turn(m):
                pe.wait_ge(max_parts, 2 * m + 2)
                for half in range(NH):
                    last = nc.tensor.matmul(max_ps[:, 0, half * P:(half + 1) * P], max_cols[:, half, :], ident16[:],
                                            start=True, stop=True)
                last.then_inc(max_rows, 1)

            def score_unit(m, u, par, first=False):
                if u == 0:
                    pe.wait_ge(max_free, 5 * m + 5)
                if not first or u >= 2:
                    pe.wait_ge(exps, UNITS * m + (u - 1))
                s0, k, rows = unit_slots(u)
                for s in ([s0, s0 + 2, s0 + 1, s0 + 3] if k == 4 else [s0]):
                    r, col, n = slot_column(s)
                    at = s - s0
                    last = nc.tensor.matmul(sc_ps[u % 2][0:n, at // 2, (at % 2) * S:(at % 2 + 1) * S],
                                            k_sb[64 * r:64 * r + KR, par, col:col + n], q_max[64 * r:64 * r + KR, :],
                                            start=True, stop=True)
                last.then_inc(scores, 1)

            def value_slot(n, half, s, par):
                rows = slot_token(s)[1]
                if half == 0 and s % 4 == 0:
                    u = s // 4
                    if u % 2 == 0:
                        pe.wait_ge(lo_dve, 2 * n + (u // 2 + 1))
                    else:
                        pe.wait_ge(lo_pool, 2 * n + (u // 2 + 1))
                if half == 0 and s == 0:
                    pe.wait_ge(v_cols, n + 1)
                if s == 0:
                    pe.wait_ge(val_read[half], n)
                hi = p_hi[0:rows, par, s, half * P:(half + 1) * P]
                lo = p_lo[0:rows, par, s, half * P:(half + 1) * P]
                x_hi = aug[0:rows, par, 0, s, 0:W_AUG]
                x_lo = aug[0:rows, par, 1, s, 0:W_AUG]
                acc = val_ps[half][:, 0:W_AUG]
                nc.tensor.matmul(acc, hi, x_hi, start=(s == 0), stop=False)
                nc.tensor.matmul(acc, hi, x_lo, start=False, stop=False)
                last = nc.tensor.matmul(acc, lo, x_hi, start=False, stop=(s == NT - 1))
                if s == NT - 1:
                    last.then_inc(val_done[half], 1)

            def post_turn_probs(b):
                pe.wait_ge(post_dve, POST_DVE * b + POST_AT["text"])
                for half in range(NH):
                    last = nc.tensor.transpose(max_ps[0:HEADS * IP, 0, half * P:(half + 1) * P],
                                               probs[:, half, :, :].rearrange("p h i -> p (h i)"), ident32[:])
                last.then_inc(post_pe, 1)

            def post_turn_out(b):
                pe.wait_ge(post_dve, POST_DVE * b + POST_AT["probsT"])
                pe.wait_ge(post_pool, 2 * b + 2)
                for g in range(MG):
                    for half in range(NH):
                        dst = max_ps[0:CG, 0, (g * NH + half) * P:(g * NH + half + 1) * P]
                        nc.tensor.matmul(dst, text[:, half, g * CG:(g + 1) * CG], ident32[:], start=True, stop=False)
                        last = nc.tensor.matmul(dst, ip_values_b[:, g * CG:(g + 1) * CG], probsT[:, half, :],
                                                start=False, stop=True)
                last.then_inc(post_pe, 1)

            def post_project(b):
                pe.wait_ge(post_dve, POST_DVE * b + POST_AT["oT"])
                for half in range(NH):
                    dst = max_ps[:, 0, half * C:(half + 1) * C]
                    for g in range(MG):
                        nc.tensor.matmul(dst, oT[:, g, half * P:(half + 1) * P], wout_sb[:, g, :], start=(g == 0),
                                         stop=False)
                    last = nc.tensor.matmul(dst, ones_sb[0:1, :], bout_sb[:], start=False, stop=True)
                last.then_inc(post_pe, 1)

            def step(g, par, score=True, maxima=True, post=None):
                n = g * 2 + par
                post = post or {}
                between = {}
                if score:
                    for place, u in ((0, 0), (1, 1), (6, 2), (11, 3)):
                        between[place] = lambda u=u: score_unit(n + 1, u, 1 - par)
                if maxima:
                    for place, c in ((2, 0), (7, 1), (12, 2), (17, 3)):
                        between[place] = lambda c=c: max_chunk(n + 2, g + 1, c, par)
                    between[22] = lambda: max_turn(n + 2)
                for half in range(NH):
                    for s in range(NT):
                        value_slot(n, half, s, par)
                        place = half * NT + s
                        between.get(place, lambda: None)()
                        post.get(place, lambda: None)()

            for m in range(2):
                for c in range(4):
                    max_chunk(m, 0, c, m)
                max_turn(m)
                if m == 0:
                    for u in range(UNITS):
                        score_unit(0, u, 0, first=True)
            step(0, 0)
            step(0, 1)
            with pe.Fori(0, B - 1) as b:
                with pe.Fori(0, HEADS // 2 - 1) as j:
                    g = b * (HEADS // 2) + j + 1
                    step(g, 0)
                    step(g, 1)
                g = b * (HEADS // 2) + HEADS // 2

                def after_reads(m, c, what, b):
                    pe.wait_ge(max_free, 5 * m + c)
                    what(b)

                m = g * 2 + 2
                step(g, 0, post={25: lambda: after_reads(m, 5, post_turn_probs, b),
                                 })
                pe.wait_ge(post_dve, POST_DVE * b + POST_AT["probsT"])
                step(g, 1, post={4: lambda: after_reads(m + 1, 1, post_turn_out, b),
                                 6: lambda: pe.wait_ge(post_dve, POST_DVE * b + POST_AT["oT"]),
                                 9: lambda: after_reads(m + 1, 2, post_project, b),
                                 11: lambda: pe.wait_ge(post_dve, POST_DVE * b + POST_AT["y"])})
            with pe.Fori(0, HEADS // 2 - 2) as j:
                g = j + ((B - 1) * (HEADS // 2) + 1)
                step(g, 0)
                step(g, 1)
            step(BH // 2 - 1, 0, maxima=False)
            step(BH // 2 - 1, 1, score=False, maxima=False)
            for stage in (post_turn_probs, post_turn_out, post_project):
                stage(B - 1)


def kernel(x, ctx_2048, fside_S_0, L0_xattn_W_q, L0_xattn_W_k, L0_xattn_W_v, L0_xattn_W_k_ip, L0_xattn_W_v_ip,
           L0_xattn_W_out, L0_xattn_b_out):
    import numpy as np
    import concourse.bacc as bacc
    from concourse import mybir as mb
    from concourse.bass_utils import run_bass_kernel_spmd

    x, ctx = np.asarray(x), np.asarray(ctx_2048)
    B, S, C = x.shape
    heads, ip = HEADS, IP
    channel_head = np.arange(C) // DH
    arrays = {
        "x": x,
        "xT": x.reshape(B * S, C).T,
        "ctx": ctx,
        "ctxT": ctx.transpose(0, 2, 1),
        "smask": np.asarray(fside_S_0).reshape(S // P, P).T,
        "Wq": L0_xattn_W_q,
        "Wk": L0_xattn_W_k,
        "Wv": L0_xattn_W_v,
        "Wkip": L0_xattn_W_k_ip,
        "Wvip": L0_xattn_W_v_ip,
        "Wout": L0_xattn_W_out,
        "bout": L0_xattn_b_out,
        "ident": np.eye(P, dtype=np.float32),
        "bdk_mask": (channel_head[:C // 2, None] == np.arange(heads // 2)[None, :]).astype(np.float32),
        "bdv_mask": (np.repeat(np.arange(heads), ip)[:, None] == channel_head[None, :]).astype(np.float32),
    }
    arrays = {f"in_{k}": np.ascontiguousarray(v) for k, v in arrays.items()}
    nc = bacc.Bacc("TRN2", target_bir_lowering=False, num_devices=1)
    args = [nc.dram_tensor(k, v.shape, mb.dt.from_np(v.dtype), kind="ExternalInput").ap() for k, v in arrays.items()]
    out = nc.dram_tensor("out_y", (B, S, C), mb.dt.float32, kind="ExternalOutput").ap()
    xattn(nc, *args, out)
    r = run_bass_kernel_spmd(nc, [arrays], core_ids=[0])
    return r.results[0]["out_y"]
```

```python
from contextlib import ExitStack

import concourse.bass as bass
from concourse import mybir

ALU = mybir.AluOpType
ACT = mybir.ActivationFunctionType
F16 = mybir.dt.float16
F32 = mybir.dt.float32
AX = mybir.AxisListType

P = 128
LN2 = 0.6931471805599453
EPS = 1e-12
SEM_SCALE = 0.5
X_SCALE = 64.0
K_SCALE = 32.0
HEADS = 20
IP = 4
DH = 8


def xattn(nc, x, xT, ctx, ctxT, smask, Wq, Wk, Wv, Wkip, Wvip, Wout, bout, ip_tokens, ident, bdk_mask, bdv_mask, out):
    B, S, C = x.shape
    T = ctx.shape[1] - IP
    E = ctx.shape[2]
    NE = E // P
    NH = S // P
    BH = B * HEADS
    MG = 2
    CG = C // MG
    HG = HEADS // MG
    SOFT = DH ** -0.5
    Q_SCALE = 32.0 * SOFT
    S_SCALE = 2.0 ** -10
    P_SHIFT = 14 * LN2

    NT = (T + P - 1) // P
    TAIL = T - (NT - 1) * P
    G0 = (NT - 1) // 2 * P + TAIL
    GM = (T + 1) // 2
    MC = 400
    G1_FIRST = T - GM
    UNITS = (NT + 3) // 4
    KROWS = 3 * DH
    KR = KROWS + 2
    assert (NT - 1) % 4 == 0 and 2 * MC - 1 == GM and G0 >= GM and T - G0 == (NT - 1) // 2 * P

    def slot_token(slot):
        if slot == NT - 1:
            return (NT - 1) // 2 * P, TAIL
        u, k = divmod(slot, 4)
        return (2 * u + k, 0)[0] * P if k < 2 else G0 + (2 * u + k - 2) * P, P

    def slot_column(slot):
        t0, n = slot_token(slot)
        return (0, t0, n) if slot == NT - 1 or slot % 4 < 2 else (1, t0 - G1_FIRST, n)

    CG_IP = E
    CG_ONE = E + IP
    CG_V = CG_ONE + 2
    W_AUG = CG_V + DH
    W_RES = W_AUG - E

    k_dram = nc.dram_tensor("k_stacked", (BH, KROWS, T), F16).ap()
    q_dram = nc.dram_tensor("q_stacked", (BH, KROWS, S), F16).ap()

    with ExitStack() as st:
        def sb(name, shape, dt):
            return st.enter_context(nc.sbuf_tensor(name, shape, dt))

        def psum(name, shape, dt):
            return st.enter_context(nc.psum_tensor(name, shape, dt))

        def sem(name):
            return st.enter_context(nc.semaphore(name))

        ctx_parts = sb("ctx_parts", [P, B, 2, NT, CG_V], F16)
        v_parts = sb("v_parts", [P, 2, NT, B * C], F16)
        wout_sb = sb("wout_sb", [CG, MG, C], F32)
        bout_sb = sb("bout_sb", [1, C], F32)
        ones_sb = sb("ones_sb", [P, P], F32)
        ident32 = sb("ident32", [P, P], F32)
        ident16 = sb("ident16", [P, P], F16)
        smask_sb = sb("smask_sb", [P, NH], F32)
        x_sb = sb("x_sb", [P, B * NH, C], F32)
        ip_scores = sb("ip_scores", [P, B, HEADS, NH, IP], F32)
        ip_values = sb("ip_values", [HEADS * IP, B * C], F32)
        heads_out = sb("heads_out", [P, BH, NH, W_RES], F32)
        sem_sq = sb("sem_sq", [P, BH, NH], F32)
        half_pow = sb("half_pow", [P, HEADS * NH], F32)
        k_sb = sb("k_sb", [P, 2, G0 + G0 % 2], F16)
        q_sb = sb("q_sb", [P, 2, S], F16)
        q_max = sb("q_max", [P, S], F16)
        max_cols = sb("max_cols", [P, NH, P], F16)
        aug = sb("aug", [P, 2, 2, NT, W_AUG], F16)
        p_hi = sb("p_hi", [P, 2, NT, S], F16)
        p_lo = sb("p_lo", [P, 2, NT, S], F16)
        p_32 = sb("p_32", [P, NT, S], F32)
        mx = sb("mx", [P, NH, 2], F32)
        mx1 = sb("mx1", [P, NH], F32)
        den = sb("den", [P, HEADS, NH], F32)
        eps_sq = sb("eps_sq", [P, HEADS, NH], F32)
        guard = sb("guard", [P, HEADS, NH], F32)
        rnorm = sb("rnorm", [P, HEADS, NH], F32)
        rden = sb("rden", [P, HEADS, NH], F32)
        fused = sb("fused", [P, HEADS, NH, IP], F32)
        fmax = sb("fmax", [P, HEADS, NH], F32)
        probs = sb("probs", [P, NH, HEADS, IP], F32)
        text = sb("text", [P, NH, C], F32)
        probsT = sb("probsT", [HEADS * IP, NH, P], F32)
        ip_values_b = sb("ip_values_b", [HEADS * IP, C], F32)
        fsum = sb("fsum", [P, HEADS, NH], F32)
        rsum = sb("rsum", [P, HEADS, NH], F32)
        oT = sb("oT", [P, MG, S], F32)

        max_ps = psum("max_ps", [P, 2, 512], F32)
        sc_ps = [psum(f"sc_ps{i}", [P, 2, 512], F32) for i in range(2)]
        post_ps = sc_ps[1][:, 1, :]
        val_ps = [psum(f"val_ps{i}", [P, 512], F32) for i in range(2)]

        q_in = sem("q_in")
        w_in = sem("w_in")
        x_in = sem("x_in")
        ip_in = sem("ip_in")
        wkv_in = sem("wkv_in")
        c_in = [[sem(f"c_in{b}_{h}") for h in range(2)] for b in range(B)]
        cT_in = [[sem(f"cT_in{b}_{c}") for c in range(2)] for b in range(B)]
        init = sem("init")
        pro_pe = sem("pro_pe")
        pro_act = sem("pro_act")
        pro_dve = sem("pro_dve")
        pro_pool = sem("pro_pool")
        pool_init = sem("pool_init")
        dve_init = sem("dve_init")
        unit_hi = sem("unit_hi")
        pool_ip = sem("pool_ip")
        post_ipv = sem("post_ipv")
        q_out = sem("q_out")
        k_out = [sem(f"k_out{g}") for g in range(MG)]
        aug_in = [[sem(f"aug_in{par}_{i}") for i in range(2)] for par in range(2)]
        kq_in = [sem(f"kq_in{i}") for i in range(2)]
        max_scores = sem("max_scores")
        max_free = sem("max_free")
        max_parts = sem("max_parts")
        max_one = sem("max_one")
        max_rows = sem("max_rows")
        scores = sem("scores")
        exps = sem("exps")
        lo_dve = sem("lo_dve")
        lo_pool = sem("lo_pool")
        v_cols = sem("v_cols")
        val_done = [sem(f"val_done{i}") for i in range(NH)]
        val_read = [sem(f"val_read{i}") for i in range(NH)]
        post_dve = sem("post_dve")
        post_act = sem("post_act")
        post_pool = sem("post_pool")
        post_pe = sem("post_pe")
        y_out = sem("y_out")

        def view(tensor, start, shape, dt):
            flat = tensor[0:shape[0]]
            size = shape[1] * shape[2] * (2 if dt == F32 else 1)
            flat = flat.rearrange("p a b c -> p (a b c)") if len(flat.shape) == 4 else flat.rearrange("p a b c d -> p (a b c d)")
            part = flat[:, start:start + size]
            part = part.bitcast(F32) if dt == F32 else part
            return part.rearrange("p (a b) -> p a b", a=shape[1])

        TALL = T + IP
        W_SCALE = 64.0
        PART = NE * TALL
        c_rows = p_32
        cT_raw = view(aug, 2 * NT * W_AUG, [P, NE, TALL], F32)
        kh = view(aug, 0, [CG, MG, TALL], F16)
        kl = view(aug, MG * TALL, [CG, MG, TALL], F16)
        cT = [[view(t, part * PART, [P, NE, TALL], F16) for part in range(2)] for t in (p_hi, p_lo)]
        wk_raw = v_parts[:, 0, 0, :].bitcast(F32).rearrange("p (e c) -> p e c", e=NE)
        wv_raw = v_parts[:, 0, 1, :].bitcast(F32).rearrange("p (e c) -> p e c", e=NE)
        xT_sb = heads_out[0:CG].rearrange("p a b c -> p (a b c)")[:, 0:MG * B * S].rearrange("p (g t) -> p g t", g=MG)
        wq_sb = k_sb[0:CG].rearrange("p a b -> p (a b)")[:, 0:2 * MG * C].bitcast(F32).rearrange("p (g c) -> p g c", g=MG)
        qh = x_sb[0:CG].rearrange("p a b -> p (a b)").bitcast(F16)[:, 0:MG * B * S].rearrange("p (g t) -> p g t", g=MG)
        wkip_sb = text[:]
        wvip_sb = oT[:, :, 0:C]
        ql = sb("ql", [CG, MG, B * S], F16)
        qT_sb = sb("qT_sb", [CG, MG, B * S], F32)
        wk_sb = sb("wk_sb", [P, 2, NE, C], F16)
        wv_sb = sb("wv_sb", [P, 2, 2, NE, C + IP], F16)
        bdk_mask_sb = sb("bdk_mask_sb", [CG, HG], F32)
        bdv_mask_sb = sb("bdv_mask_sb", [HEADS * IP, C], F32)
        ip_cols = sb("ip_cols", [P, NE, B * IP], F32)
        ip_sq = sb("ip_sq", [P, NE, B * IP], F32)
        ip_rep = sb("ip_rep", [P, NE, B, HEADS * IP], F32)
        ip_unit = sb("ip_unit", [P, NE, B * IP], F32)
        ip_n2 = sb("ip_n2", [P, B * IP], F32)
        ip_rn = sb("ip_rn", [P, B * IP], F32)
        kipT = sb("kipT", [CG, MG, B * IP], F32)
        bdk = ip_rep[0:CG].rearrange("p e b h -> p (e b h)")[:, 0:MG * B * HG * IP].rearrange(
            "p (g b h i) -> p g b h i", g=MG, b=B, h=HG)

        block = st.enter_context(nc.Block())

        N_WIN = 6

        V_PER = 3
        V_USES = (NT + V_PER - 1) // V_PER
        K_USES = 2 * MG
        ORDER = """w, cols 0 0, k 0 0, k 0 1, cols 0 1, k 0 2, k 0 3, norms, ipk, ipv 0, ipv 1, blocks, unit 0,
            rows 0 0, v 0 0, q 0, v 0 1, rows 0 1, q 1, v 0 2, cols 1 0, ips 0, v 0 3, ips 1, v 0 4, cols 1 1,
            unit 1, k 1 0, rows 1 0, v 1 0, k 1 1, v 1 1, k 1 2, rows 1 1, v 1 2, k 1 3, cols 2 0, v 1 3, v 1 4, cols 2 1,
            unit 2, k 2 0, rows 2 0, v 2 0, m 0 0, k 2 1, v 2 1, m 0 1, k 2 2, rows 2 1, v 2 2, m 0 2, k 2 3,
            cols 3 0, v 2 3, m 0 3, turn 0, v 2 4, cols 3 1,
            unit 3, k 3 0, rows 3 0, v 3 0, k 3 1, m 1 0, k 3 2, rows 3 1, v 3 1, m 1 1, k 3 3,
            v 3 2, m 1 2, s 0, s 1, v 3 3, m 1 3, turn 1, s 2, v 3 4, s 3"""
        ORDER = [tuple(int(w) if w.isdigit() else w for w in step.split()) for step in ORDER.split(",")]

        def tally(order):
            return {name: i + 1 for i, name in enumerate(order)}

        def share(*kinds):
            return tally([step for step in ORDER if step[0] in kinds])

        PE_AT = share("k", "v", "norms", "ipk", "ipv", "q", "ips")
        ACT_AT = share("w", "cols", "rows", "k", "v", "q", "ips")
        DVE_AT = share("w", "cols", "rows", "k", "v", "unit", "norms", "ipk", "ipv", "blocks", "q")
        POOL_AT = share("rows")
        V_LAST = V_USES - 1

        def v_use(i):
            s0 = V_PER * i
            k = min(V_PER, NT - s0)
            rows = P if s0 + k < NT else TAIL
            assert rows == P or k == 1
            return s0, k, rows, val_ps[i % 2][0:rows, 0:k * (C + IP)].rearrange("p (s c) -> p s c", s=k)

        AUG_SLOTS = (slice(0, 6), slice(6, NT))
        ROWS_OF = (slice(0, 6), slice(6, NT))

        POST_AT = tally(["den", "eps", "guard", "rden", "dots", "fused", "fmax", "shifted", "fsum", "rsum", "masked",
                         "probs", "text", "probsT", "oT", "y"])
        POST_DVE = len(POST_AT)
        POST_OWN = POST_AT["text"]
        POST_END = POST_DVE * B + POST_OWN
        LATE = 2

        def unit_slots(u):
            return (4 * u, min(4, NT - 4 * u), P if u < UNITS - 1 else TAIL)

        def lo_unit(engine, u, par):
            s0, k, rows = unit_slots(u)
            return engine.tensor_tensor(p_lo[0:rows, par, s0:s0 + k, :], p_32[0:rows, s0:s0 + k, :],
                                        p_hi[0:rows, par, s0:s0 + k, :], ALU.subtract)


        def post_base(k):
            return POST_DVE * (B - 1) + POST_OWN if isinstance(k, int) and k == B else k * POST_DVE

        @block.sync
        def _(sp):
            def head_load(n, par):
                for g in range(2):
                    cols = slice(0, G0) if g == 0 else slice(G1_FIRST, T)
                    w = G0 if g == 0 else GM
                    sp.dma_start(k_sb[64 * g:64 * g + KROWS, par, 0:w],
                                 k_dram[bass.ds(n, 1), :, cols].rearrange("o r t -> (o r) t")).then_inc(kq_in[par], 16)
                    sp.dma_start(q_sb[64 * g:64 * g + KROWS, par, :],
                                 q_dram[bass.ds(n, 1), :, :].rearrange("o r t -> (o r) t")).then_inc(kq_in[par], 16)

            def aug_load(b, par):
                for i, slots in enumerate(AUG_SLOTS):
                    for part in range(2):
                        sp.dma_start(aug[:, par, part, slots, 0:CG_V],
                                     ctx_parts[:, bass.ds(b, 1), part, slots, :].rearrange("p o s c -> p (o s) c")
                                     ).then_inc(aug_in[par][i], 16)

            def rows_load(b, h):
                for s in range(NT)[ROWS_OF[h]]:
                    t0, n = slot_token(s)
                    sp.dma_start(c_rows[0:n, s, :], ctx[b, t0:t0 + n, :]).then_inc(c_in[b][h], 16)

            def columns_load(b):
                for c in range(2):
                    cols = slice(c * 2 * MC, 2 * MC if c == 0 else TALL)
                    sp.dma_start(cT_raw[:, :, cols], ctxT[b].rearrange("(e p) t -> p e t", p=P)[:, :, cols]
                                 ).then_inc(cT_in[b][c], 16)

            def keys_store(b):
                for mg in range(MG):
                    sp.wait_ge(pro_dve, DVE_AT["k", b, 2 + mg])
                    for r, part in enumerate([kh, kl, kh]):
                        sp.dma_start(k_dram[b * HEADS + mg * HG:b * HEADS + (mg + 1) * HG, r * DH:(r + 1) * DH, :],
                                     part[:, mg, 0:T]).then_inc(k_out[mg], 16)

            def rows_next(b):
                for h in range(2):
                    sp.wait_ge(pro_pool, POOL_AT["rows", b - 1, h])
                    rows_load(b, h)

            columns_load(0)
            sp.wait_ge(pro_dve, DVE_AT["w",])
            for h in range(2):
                rows_load(0, h)
            sp.wait_ge(pro_dve, DVE_AT["cols", 0, 1])
            columns_load(1)
            keys_store(0)
            rows_next(1)
            sp.wait_ge(pro_dve, DVE_AT["cols", 1, 1])
            columns_load(2)
            keys_store(1)
            for mg in range(MG):
                sp.wait_ge(k_out[mg], 16 * 3)
            sp.wait_ge(q_out, 16 * 3 * MG * B)
            sp.wait_ge(pool_init, 2)
            head_load(0, 0)
            rows_next(2)
            head_load(1, 1)
            sp.wait_ge(pro_dve, DVE_AT["cols", 2, 1])
            columns_load(3)
            keys_store(2)
            rows_next(3)
            sp.wait_ge(pro_dve, DVE_AT["cols", 3, 1])
            aug_load(0, 1)
            keys_store(3)
            for mg in range(MG):
                sp.wait_ge(k_out[mg], 16 * 3 * B)
            aug_load(0, 0)
            sp.wait_ge(scores, UNITS)
            head_load(2, 0)

            def step(n, par):
                sp.wait_ge(scores, UNITS * (n + 2))
                head_load(n + 3, 1 - par)

            with sp.Fori(0, B - 1) as b:
                with sp.Fori(0, HEADS // 2 - 1) as j:
                    n = b * HEADS + j * 2
                    step(n, 0)
                    step(n + 1, 1)
                n = b * HEADS + (HEADS - 2)
                step(n, 0)
                sp.wait_ge(val_done[1], n + 1)
                aug_load(b + 1, 0)
                step(n + 1, 1)
                sp.wait_ge(val_done[1], n + 2)
                aug_load(b + 1, 1)
            with sp.Fori(0, HEADS // 2 - 2) as j:
                n = j * 2 + (B - 1) * HEADS
                step(n, 0)
                step(n + 1, 1)
            step(BH - 4, 0)

        @block.gpsimd
        def _(pool):
            nc.gpsimd.memset(ctx_parts[:, :, :, NT - 1, 0:CG_ONE], 0.0)
            nc.gpsimd.memset(v_parts[:, :, NT - 1, :], 0.0)
            nc.gpsimd.memset(q_sb[:], 0.0)
            nc.gpsimd.memset(max_cols[:], 0.0)
            nc.gpsimd.memset(half_pow[:], -0.5)
            nc.gpsimd.memset(ctx_parts[:, :, 0, :, CG_ONE:CG_ONE + 1], X_SCALE)
            nc.gpsimd.memset(ctx_parts[:, :, 0, :, CG_ONE + 1:CG_V], 0.0)
            nc.gpsimd.memset(ctx_parts[:, :, 1, :, CG_ONE:CG_V], 0.0).then_inc(pool_init, 1)
            pool.wait_ge(pro_dve, DVE_AT["norms",])
            pool.wait_ge(pool_init, 1)
            nc.gpsimd.tensor_tensor(ip_rn[:], ip_n2[:], half_pow[:, 0:B * IP], ALU.pow).then_inc(pool_ip, 1)
            pool.wait_ge(pool_ip, 1)
            nc.gpsimd.tensor_tensor(ip_unit[:], ip_cols[:], ip_rn[:].unsqueeze(1).to_broadcast([P, NE, B * IP]),
                                    ALU.mult).then_inc(pool_ip, 1)
            for b in range(B):
                for h in range(2):
                    if (b, h) == (1, 0):
                        pool.wait_ge(pro_pe, PE_AT["q", 1])
                        nc.gpsimd.memset(k_sb[:], -K_SCALE * 32.0).then_inc(pool_init, 1)
                    pool.wait_ge(pro_act, ACT_AT["rows", b, h])
                    full = slice(ROWS_OF[h].start, min(ROWS_OF[h].stop, NT - 1))
                    last = nc.gpsimd.tensor_tensor(ctx_parts[:, b, 1, full, 0:E], c_rows[:, full, :],
                                                   ctx_parts[:, b, 0, full, 0:E], ALU.subtract)
                    if h == 1:
                        last = nc.gpsimd.tensor_tensor(ctx_parts[0:TAIL, b, 1, NT - 1, 0:E], c_rows[0:TAIL, NT - 1, :],
                                                       ctx_parts[0:TAIL, b, 0, NT - 1, 0:E], ALU.subtract)
                    last.then_inc(pro_pool, 1)

            def values_of(m, par):
                nc.gpsimd.tensor_copy(aug[:, par, :, :, CG_V:W_AUG],
                                      v_parts[:, :, :, bass.ds(m * DH, DH)]).then_inc(v_cols, 1)

            def lo_parts(m, par):
                for u in (1, 3):
                    pool.wait_ge(exps, UNITS * m + (u + 1))
                    lo_unit(nc.gpsimd, u, par).then_inc(lo_pool, 1)

            def head(m, par, between=lambda: None):
                pool.wait_ge(val_done[1], m - 1)
                values_of(m, par)
                between()
                lo_parts(m, par)

            def post_pow(k, heads):
                g0, g1 = heads.start * NH, heads.stop * NH
                pool.wait_ge(post_dve, post_base(k) + POST_AT["guard"])
                nc.gpsimd.tensor_tensor(rnorm[:].rearrange("p h n -> p (h n)")[:, g0:g1],
                                        guard[:].rearrange("p h n -> p (h n)")[:, g0:g1],
                                        half_pow[:, g0:g1], ALU.pow).then_inc(post_pool, 1)

            def post_values(b):
                nc.gpsimd.tensor_copy(ip_values_b[:], ip_values[:, bass.ds(b * C, C)]).then_inc(post_ipv, 1)

            pool.wait_ge(pro_dve, DVE_AT["v", 3, V_LAST])
            for mg in range(MG):
                pool.wait_ge(k_out[mg], 16 * 3 * B)
            for m in range(2):
                values_of(m, m)
                lo_parts(m, m)
            with pool.Fori(0, B - 1) as b:
                with pool.Fori(0, HEADS // 2 - 1) as j:
                    m = b * HEADS + j * 2 + 2
                    head(m, 0)
                    head(m + 1, 1)
                m = b * HEADS + HEADS
                head(m, 0)
                head(m + 1, 1, between=lambda: post_pow(b, range(HEADS)))
                post_values(b)
            with pool.Fori(0, HEADS // 2 - 2) as j:
                m = j * 2 + ((B - 1) * HEADS + 2)
                head(m, 0)
                head(m + 1, 1)
            head(BH - 2, 0)
            head(BH - 1, 1, between=lambda: post_pow(B - 1, range(HEADS - LATE)))
            post_values(B - 1)
            post_pow(B, range(HEADS - LATE, HEADS))

        @block.scalar
        def _(act):
            act.dma_start(wk_raw, Wk.rearrange("(e p) n -> p e n", p=P)).then_inc(wkv_in, 16)
            act.dma_start(wv_raw, Wv.rearrange("(e p) n -> p e n", p=P)).then_inc(wkv_in, 16)
            act.dma_start(ip_cols[:], ip_tokens.rearrange("(e p) t -> p e t", p=P)).then_inc(ip_in, 16)
            act.dma_start(wkip_sb, Wkip.rearrange("(e p) n -> p e n", p=P)).then_inc(ip_in, 16)
            act.dma_start(wvip_sb, Wvip.rearrange("(e p) n -> p e n", p=P)).then_inc(ip_in, 16)
            act.dma_start(bdk_mask_sb[:], bdk_mask).then_inc(w_in, 16)
            act.dma_start(bdv_mask_sb[:], bdv_mask).then_inc(w_in, 16)
            act.dma_start(xT_sb, xT.rearrange("(g c) t -> c g t", g=MG)).then_inc(q_in, 16)
            act.dma_start(wq_sb, Wq.rearrange("(g c) n -> c g n", g=MG)).then_inc(q_in, 16)
            act.dma_start(ident32[:], ident).then_inc(w_in, 16)
            act.dma_start(wout_sb[:], Wout.rearrange("(g c) n -> c g n", g=MG)).then_inc(w_in, 16)
            act.dma_start(bout_sb[:], bout.rearrange("(o c) -> o c", o=1)).then_inc(w_in, 16)
            act.dma_start(smask_sb[:], smask).then_inc(w_in, 16)

            def weights_hi():
                act.wait_ge(wkv_in, 32)
                nc.scalar.activation(wk_sb[:, 0], wk_raw, ACT.Copy, scale=W_SCALE)
                for i in range(2):
                    last = nc.scalar.activation(wv_sb[:, i, 0, :, 0:C], wv_raw, ACT.Copy, scale=W_SCALE)
                return last

            def columns_hi(b, c):
                act.wait_ge(cT_in[b][c], 16)
                if b >= 2:
                    act.wait_ge(pro_pe, PE_AT["v", b - 2, V_LAST])
                cols = slice(c * 2 * MC, 2 * MC if c == 0 else TALL)
                return nc.scalar.activation(cT[b % 2][0][:, :, cols], cT_raw[:, :, cols], ACT.Copy, scale=X_SCALE)

            def rows_hi(b, h):
                act.wait_ge(pro_dve, DVE_AT["rows", b, h])
                if (b, h) == (0, 0):
                    act.wait_ge(pool_init, 1)
                full = slice(ROWS_OF[h].start, min(ROWS_OF[h].stop, NT - 1))
                last = nc.scalar.activation(ctx_parts[:, b, 0, full, 0:E], c_rows[:, full, :], ACT.Copy)
                if h == 1:
                    last = nc.scalar.activation(ctx_parts[0:TAIL, b, 0, NT - 1, 0:E], c_rows[0:TAIL, NT - 1, :],
                                                ACT.Copy)
                return last

            def key_hi(b, i):
                c, mg = divmod(i, MG)
                act.wait_ge(pro_pe, PE_AT["k", b, i])
                if b >= 1 and c == 0:
                    act.wait_ge(k_out[mg], 16 * 3 * b)
                return nc.scalar.activation(kh[:, mg, 2 * MC * c:2 * MC * (c + 1)].rearrange("p (a t) -> p a t", a=2),
                                            sc_ps[mg][0:CG, :, 0:MC], ACT.Copy, scale=K_SCALE / (X_SCALE * W_SCALE))

            def value_hi(b, i):
                s0, k, rows, src = v_use(i)
                act.wait_ge(pro_pe, PE_AT["v", b, i])
                if (b, i) == (0, 0):
                    act.wait_ge(pro_dve, DVE_AT["w",])
                nc.scalar.activation(v_parts[0:rows, 0, s0:s0 + k, b * C:(b + 1) * C], src[:, :, 0:C], ACT.Copy,
                                     scale=1.0 / W_SCALE)
                return nc.scalar.activation(ctx_parts[0:rows, b, 0, s0:s0 + k, CG_IP:CG_ONE], src[:, :, C:C + IP],
                                            ACT.Copy, scale=1.0 / W_SCALE)

            def queries_hi(mg):
                act.wait_ge(pro_pe, PE_AT["q", mg])
                src = sc_ps[mg][0:CG, :, :].rearrange("c a t -> c (a t)")
                nc.scalar.activation(qT_sb[:, mg, :], src, ACT.Copy)
                return nc.scalar.activation(qh[:, mg, :], src, ACT.Copy, scale=Q_SCALE)

            def queries_store(mg):
                act.wait_ge(pro_dve, DVE_AT["q", mg])
                for r, part in enumerate([qh, qh, ql]):
                    for b in range(B):
                        act.dma_start(q_dram[b * HEADS + mg * HG:b * HEADS + (mg + 1) * HG, r * DH:(r + 1) * DH, :],
                                      part[:, mg, b * S:(b + 1) * S]).then_inc(q_out, 16)

            def ip_scores_out(i):
                act.wait_ge(pro_pe, PE_AT["ips", i])
                for b in (2 * i, 2 * i + 1):
                    c0 = (b % 2) * NH * HEADS * IP
                    last = nc.scalar.activation(
                        ip_scores[:, b, :, :, :], max_ps[:, i, c0:c0 + NH * HEADS * IP].rearrange(
                            "p (a h i) -> p h a i", a=NH, h=HEADS), ACT.Copy, scale=SOFT)
                return last

            def exp_unit(m, u, par, first=False):
                act.wait_ge(scores, UNITS * m + (u + 1))
                if not first:
                    if u % 2 == 0:
                        act.wait_ge(lo_dve, 2 * m - 2 + (u // 2 + 1))
                    else:
                        act.wait_ge(lo_pool, 2 * m - 2 + (u // 2 + 1))
                s0, k, rows = unit_slots(u)
                src = sc_ps[u % 2][0:rows, :, :].rearrange("p a t -> p (a t)")[:, 0:k * S]
                nc.scalar.activation(p_32[0:rows, s0:s0 + k, :].rearrange("p s q -> p (s q)"), src, ACT.Exp,
                                     bias=P_SHIFT, scale=S_SCALE)
                nc.scalar.activation(p_hi[0:rows, par, s0:s0 + k, :].rearrange("p s q -> p (s q)"), src, ACT.Exp,
                                     bias=P_SHIFT, scale=S_SCALE).then_inc(exps, 1)

            def read_values(n, half):
                act.wait_ge(val_done[half], n + 1)
                nc.scalar.activation(val_ps[half][:, 0:E], val_ps[half][:, 0:E], ACT.Square,
                                     accum_out=sem_sq[:, bass.ds(n, 1), half])
                nc.scalar.activation(heads_out[:, bass.ds(n, 1), half, :].rearrange("p o c -> p (o c)"),
                                     val_ps[half][:, E:W_AUG], ACT.Copy).then_inc(val_read[half], 1)

            def post_exp(k, heads=range(HEADS)):
                act.wait_ge(post_dve, post_base(k) + POST_AT["shifted"])
                part = fused[:, heads.start:heads.stop].rearrange("p h n i -> p (h n i)")
                nc.scalar.activation(part, part, ACT.Exp).then_inc(post_act, 1)

            def store(b):
                act.wait_ge(post_dve, post_base(b + 1) if not isinstance(b, int) else POST_END)
                act.dma_start(out[bass.ds(b, 1), :, :].rearrange("o (h p) c -> p (o h) c", p=P),
                              x_sb[:, bass.ds(b * NH, NH), :]).then_inc(y_out, 16)

            def step(n, par, has_next=True, post_b=None):
                if has_next:
                    act.wait_ge(val_done[1], n)
                    exp_unit(n + 1, 0, 1 - par)
                if post_b is not None:
                    post_exp(*post_b)
                if has_next:
                    exp_unit(n + 1, 1, 1 - par)
                    exp_unit(n + 1, 2, 1 - par)
                read_values(n, 0)
                if has_next:
                    exp_unit(n + 1, 3, 1 - par)
                read_values(n, 1)

            parts = {"w": weights_hi, "cols": columns_hi, "rows": rows_hi, "k": key_hi, "v": value_hi,
                     "q": queries_hi, "ips": ip_scores_out}
            for name in ORDER:
                if name[0] in parts:
                    parts[name[0]](*name[1:]).then_inc(pro_act, 1)
                if name == ("v", 0, 2):
                    queries_store(0)
                if name == ("v", 0, 3):
                    queries_store(1)
                if name == ("k", 2, 0):
                    act.wait_ge(q_out, 16 * 3 * MG * B)
                    act.dma_start(x_sb[:], x.rearrange("b (h p) c -> p (b h) c", p=P)).then_inc(x_in, 16)
                if name[0] == "s":
                    if name[1] == 0:
                        act.wait_ge(pro_pool, POOL_AT["rows", B - 1, 1])
                        act.wait_ge(pro_pe, PE_AT["v", B - 2, V_LAST])
                    exp_unit(0, name[1], 0, first=True)
            step(0, 0)
            step(1, 1)
            with act.Fori(0, B - 1) as b:
                with act.Fori(0, HEADS // 2 - 1) as j:
                    n = b * HEADS + j * 2 + 2
                    step(n, 0)
                    step(n + 1, 1)
                n = b * HEADS + HEADS
                step(n, 0)
                step(n + 1, 1, post_b=(b,))
                store(b)
            with act.Fori(0, HEADS // 2 - 2) as j:
                n = j * 2 + ((B - 1) * HEADS + 2)
                step(n, 0)
                step(n + 1, 1)
            step(BH - 2, 0)
            step(BH - 1, 1, has_next=False, post_b=(B - 1, range(HEADS - LATE)))
            post_exp(B, range(HEADS - LATE, HEADS))
            store(B - 1)
            act.wait_ge(y_out, 16 * B)

        @block.vector
        def _(dve):
            def weights_lo():
                dve.wait_ge(pro_act, ACT_AT["w",])
                for out_, raw, hi in [(wk_sb[:, 1], wk_raw, wk_sb[:, 0])] + [
                        (wv_sb[:, i, 1, :, 0:C], wv_raw, wv_sb[:, i, 0, :, 0:C]) for i in range(2)]:
                    last = nc.vector.scalar_tensor_tensor(out=out_, in0=raw, scalar=W_SCALE, in1=hi, op0=ALU.mult,
                                                          op1=ALU.subtract)
                return last

            def columns_lo(b, c):
                dve.wait_ge(pro_act, ACT_AT["cols", b, c])
                cols = slice(c * 2 * MC, 2 * MC if c == 0 else TALL)
                return nc.vector.scalar_tensor_tensor(out=cT[b % 2][1][:, :, cols], in0=cT_raw[:, :, cols],
                                                      scalar=X_SCALE, in1=cT[b % 2][0][:, :, cols], op0=ALU.mult,
                                                      op1=ALU.subtract)

            def rows_scale(b, h):
                dve.wait_ge(c_in[b][h], 16 * len(range(NT)[ROWS_OF[h]]))
                full = slice(ROWS_OF[h].start, min(ROWS_OF[h].stop, NT - 1))
                last = nc.vector.tensor_scalar(c_rows[:, full, :], c_rows[:, full, :], X_SCALE, None, ALU.mult)
                if h == 1:
                    last = nc.vector.tensor_scalar(c_rows[0:TAIL, NT - 1, :], c_rows[0:TAIL, NT - 1, :], X_SCALE,
                                                   None, ALU.mult)
                return last

            def key_lo(b, i):
                c, mg = divmod(i, MG)
                dve.wait_ge(pro_act, ACT_AT["k", b, i])
                cols = slice(2 * MC * c, 2 * MC * (c + 1))
                return nc.vector.scalar_tensor_tensor(
                    out=kl[:, mg, cols].rearrange("p (a t) -> p a t", a=2), in0=sc_ps[mg][0:CG, :, 0:MC],
                    scalar=K_SCALE / (X_SCALE * W_SCALE), in1=kh[:, mg, cols].rearrange("p (a t) -> p a t", a=2),
                    op0=ALU.mult, op1=ALU.subtract)

            def value_lo(b, i):
                s0, k, rows, src = v_use(i)
                dve.wait_ge(pro_act, ACT_AT["v", b, i])
                nc.vector.scalar_tensor_tensor(
                    out=v_parts[0:rows, 1, s0:s0 + k, b * C:(b + 1) * C], in0=src[:, :, 0:C], scalar=1.0 / W_SCALE,
                    in1=v_parts[0:rows, 0, s0:s0 + k, b * C:(b + 1) * C], op0=ALU.mult, op1=ALU.subtract)
                return nc.vector.scalar_tensor_tensor(
                    out=ctx_parts[0:rows, b, 1, s0:s0 + k, CG_IP:CG_ONE], in0=src[:, :, C:C + IP],
                    scalar=1.0 / W_SCALE, in1=ctx_parts[0:rows, b, 0, s0:s0 + k, CG_IP:CG_ONE], op0=ALU.mult,
                    op1=ALU.subtract)

            def unit_columns(b):
                dve.wait_ge(pool_ip, 2)
                if b >= 2:
                    dve.wait_ge(pro_pe, PE_AT["v", b - 2, V_LAST])
                unit = ip_unit[:, :, b * IP:(b + 1) * IP]
                nc.vector.tensor_scalar(wv_sb[:, b % 2, 0, :, C:C + IP], unit, W_SCALE, None,
                                        ALU.mult).then_inc(unit_hi, 1)
                dve.wait_ge(unit_hi, b + 1)
                return nc.vector.scalar_tensor_tensor(out=wv_sb[:, b % 2, 1, :, C:C + IP], in0=unit, scalar=W_SCALE,
                                                      in1=wv_sb[:, b % 2, 0, :, C:C + IP], op0=ALU.mult,
                                                      op1=ALU.subtract)

            def norms():
                dve.wait_ge(pro_pe, PE_AT["norms",])
                return nc.vector.tensor_scalar(ip_n2[:], max_ps[:, 0, 0:B * IP], EPS * EPS, None, ALU.max)

            def ip_keys():
                dve.wait_ge(pro_pe, PE_AT["ipk",])
                return nc.vector.tensor_copy(kipT[:], max_ps[0:CG, 1, 0:MG * B * IP].rearrange("p (g i) -> p g i", g=MG))

            def ip_values_out(i):
                dve.wait_ge(pro_pe, PE_AT["ipv", i])
                for b in (2 * i, 2 * i + 1):
                    last = nc.vector.tensor_tensor(ip_values[:, b * C:(b + 1) * C],
                                                   val_ps[i][0:HEADS * IP, (b % 2) * C:(b % 2 + 1) * C],
                                                   bdv_mask_sb[:], ALU.mult)
                return last

            def blocks():
                dve.wait_ge(pro_dve, DVE_AT["ipk",])
                for g in range(MG):
                    last = nc.vector.tensor_tensor(
                        bdk[:, g], kipT[:, g, :].rearrange("p (b i) -> p b i", b=B).unsqueeze(2).to_broadcast(
                            [CG, B, HG, IP]),
                        bdk_mask_sb[:].unsqueeze(1).unsqueeze(3).to_broadcast([CG, B, HG, IP]), ALU.mult)
                return last

            def queries_lo(mg):
                dve.wait_ge(pro_act, ACT_AT["q", mg])
                return nc.vector.scalar_tensor_tensor(
                    out=ql[:, mg, :], in0=sc_ps[mg][0:CG, :, :].rearrange("c a t -> c (a t)"), scalar=Q_SCALE,
                    in1=qh[:, mg, :], op0=ALU.mult, op1=ALU.subtract)

            def chunk_max(m, c):
                dve.wait_ge(max_scores, 4 * m + (c + 1))
                nc.vector.tensor_reduce(mx[:, c // 2, c % 2:c % 2 + 1], max_ps[:, :, 0:MC], AX.XY,
                                        ALU.max).then_inc(max_free, 1)

            part_cols = max_cols[:].rearrange("p n (g c) -> p n g c", g=2)

            def max_parts_out(m):
                dve.wait_ge(max_free, 5 * m + 4)
                nc.vector.tensor_tensor(mx1[:], mx[:, :, 0], mx[:, :, 1], ALU.max).then_inc(max_one, 1)
                dve.wait_ge(max_one, m + 1)
                nc.vector.tensor_scalar(part_cols[:, :, :, KROWS], mx1[:].unsqueeze(2).to_broadcast([P, NH, 2]),
                                        S_SCALE, None, ALU.mult).then_inc(max_parts, 1)
                dve.wait_ge(max_parts, 2 * m + 1)
                nc.vector.scalar_tensor_tensor(out=part_cols[:, :, :, KROWS + 1],
                                               in0=mx1[:].unsqueeze(2).to_broadcast([P, NH, 2]), scalar=S_SCALE,
                                               in1=part_cols[:, :, :, KROWS], op0=ALU.mult,
                                               op1=ALU.subtract).then_inc(max_parts, 1)

            def max_to_rows(m, par, first=False):
                dve.wait_ge(max_rows, m + 1)
                if not first:
                    dve.wait_ge(scores, UNITS * m)
                nc.vector.tensor_tensor(q_max[:], q_sb[:, par, :], max_ps[:, 0, 0:S], ALU.add).then_inc(max_free, 1)

            def lo_parts(m, u, par):
                dve.wait_ge(exps, UNITS * m + (u + 1))
                lo_unit(nc.vector, u, par).then_inc(lo_dve, 1)

            def post_step(k, name, instruction):
                instruction.then_inc(post_dve, 1)
                dve.wait_ge(post_dve, post_base(k) + POST_AT[name])

            def post_norms(k, b, heads=range(HEADS)):
                h0, h = heads.start, len(heads)

                def flat(t):
                    return t[:, h0:h0 + h].rearrange("p h n -> p (h n)")

                dve.wait_ge(val_read[1], b * HEADS + (h0 + h))
                first = b * HEADS + h0
                post_step(k, "den", nc.vector.tensor_scalar(
                    flat(den), heads_out[:, bass.ds(first, h), :, IP:IP + 1].rearrange("p h n c -> p (h n c)"), 1.0,
                    None, ALU.mult))
                post_step(k, "eps", nc.vector.scalar_tensor_tensor(out=flat(eps_sq), in0=flat(den), scalar=EPS * EPS,
                                                                   in1=flat(den), op0=ALU.mult, op1=ALU.mult))
                post_step(k, "guard", nc.vector.tensor_tensor(
                    flat(guard), flat(eps_sq), sem_sq[:, bass.ds(first, h), :].rearrange("p h n -> p (h n)"),
                    ALU.max))
                post_step(k, "rden", nc.vector.reciprocal(flat(rden), flat(den)))

            def post_fused(k, b, heads=range(HEADS)):
                h0, h = heads.start, len(heads)
                part = fused[:, h0:h0 + h]
                groups = part.rearrange("p h n i -> p (h n) i")

                def over_ip(t):
                    return t[:, h0:h0 + h].rearrange("p h n -> p (h n)").unsqueeze(2).to_broadcast([P, h * NH, IP])

                dve.wait_ge(post_pool, k + 1)
                post_step(k, "dots", nc.vector.tensor_tensor(
                    groups, heads_out[:, bass.ds(b * HEADS + h0, h), :, 0:IP].rearrange("p h n c -> p (h n) c"),
                    over_ip(rnorm), ALU.mult))
                post_step(k, "fused", nc.vector.scalar_tensor_tensor(
                    out=part.rearrange("p h n i -> p (h n i)"), in0=part.rearrange("p h n i -> p (h n i)"),
                    scalar=SEM_SCALE,
                    in1=ip_scores[:, bass.ds(b, 1), h0:h0 + h, :, :].rearrange("p o h n i -> p (o h n i)"),
                    op0=ALU.mult, op1=ALU.add))
                post_step(k, "fmax", nc.vector.tensor_reduce(
                    fmax[:, h0:h0 + h].rearrange("p h n -> p (h n)"), groups, AX.X, ALU.max))
                post_step(k, "shifted", nc.vector.tensor_tensor(groups, groups, over_ip(fmax), ALU.subtract))

            def post_probs(k, b, heads=range(HEADS)):
                h0, h = heads.start, len(heads)
                part = fused[:, h0:h0 + h]
                dve.wait_ge(post_act, k + 1)
                sums = rsum[:, h0:h0 + h]
                flat_sums = sums.rearrange("p h n -> p (h n)")
                flat_fsum = fsum[:, h0:h0 + h].rearrange("p h n -> p (h n)")
                post_step(k, "fsum", nc.vector.tensor_reduce(flat_fsum, part.rearrange("p h n i -> p (h n) i"), AX.X,
                                                             ALU.add))
                post_step(k, "rsum", nc.vector.reciprocal(flat_sums, flat_fsum))
                post_step(k, "masked", nc.vector.tensor_tensor(
                    sums, sums, smask_sb[:].unsqueeze(1).to_broadcast([P, h, NH]), ALU.mult))
                post_step(k, "probs", nc.vector.tensor_tensor(
                    probs[:, :, h0:h0 + h, :].rearrange("p n h i -> p h n i"), part,
                    sums.unsqueeze(3).to_broadcast([P, h, NH, IP]), ALU.mult))
                post_step(k, "text", nc.vector.tensor_tensor(
                    text[:, :, h0 * DH:(h0 + h) * DH].rearrange("p n (h d) -> p h n d", d=DH),
                    heads_out[:, bass.ds(b * HEADS + h0, h), :, CG_V - E:W_RES],
                    rden[:, h0:h0 + h].unsqueeze(3).to_broadcast([P, h, NH, DH]), ALU.mult))

            def post_copy(k, b, count, name, out_, in_):
                dve.wait_ge(post_pe, 3 * b + count)
                post_step(k, name, nc.vector.tensor_copy(out_, in_))

            def post_probsT(k, b):
                post_copy(k, b, 1, "probsT", probsT[:].rearrange("p n s -> p (n s)"), post_ps[0:HEADS * IP, 0:S])

            def post_oT(k, b):
                post_copy(k, b, 2, "oT", oT[0:CG].rearrange("p g s -> p (g s)"), post_ps[0:CG, 0:MG * S])

            def post_y(k, b):
                x_rows = x_sb[:, bass.ds(b * NH, NH), :].rearrange("p n c -> p (n c)")
                dve.wait_ge(post_pe, 3 * b + 3)
                post_step(k, "y", nc.vector.tensor_tensor(x_rows, post_ps[:, 0:NH * C], x_rows, ALU.add))

            def step(n, par, maxima=True, post=None):
                post = post or {}

                def place(name):
                    post.get(name, lambda: None)()

                if maxima:
                    chunk_max(n + 2, 0)
                place("first")
                lo_parts(n + 1, 0, 1 - par)
                if maxima:
                    chunk_max(n + 2, 1)
                    chunk_max(n + 2, 2)
                place("middle")
                lo_parts(n + 1, 2, 1 - par)
                if maxima:
                    chunk_max(n + 2, 3)
                    max_parts_out(n + 2)
                    place("turn")
                    max_to_rows(n + 2, par)
                place("last")

            nc.vector.memset(ones_sb[:], 1.0).then_inc(dve_init, 1)
            dve.wait_ge(ip_in, 48)
            for e in range(NE):
                nc.vector.tensor_copy(
                    ip_rep[:, e, :, :].rearrange("p b (h i) -> p b h i", h=HEADS),
                    ip_cols[:, e, :].rearrange("p (b i) -> p b i", b=B).unsqueeze(2).to_broadcast([P, B, HEADS, IP]))
            nc.vector.tensor_tensor(ip_sq[:], ip_cols[:], ip_cols[:], ALU.mult).then_inc(dve_init, 1)
            parts = {"w": weights_lo, "cols": columns_lo, "rows": rows_scale, "k": key_lo, "v": value_lo,
                     "unit": unit_columns, "norms": norms, "ipk": ip_keys, "ipv": ip_values_out, "blocks": blocks,
                     "q": queries_lo}
            for name in ORDER:
                if name == ("norms",):
                    dve.wait_ge(w_in, 16 * N_WIN)
                    nc.vector.tensor_copy(ident16[:], ident32[:]).then_inc(dve_init, 1)
                if name[0] in parts:
                    parts[name[0]](*name[1:]).then_inc(pro_dve, 1)
                if name[0] == "m":
                    chunk_max(*name[1:])
                if name[0] == "turn":
                    dve.wait_ge(pool_init, 2)
                    max_parts_out(name[1])
                    max_to_rows(name[1], name[1], first=(name[1] == 0))
            lo_parts(0, 0, 0)
            lo_parts(0, 2, 0)
            dve.wait_ge(x_in, 16)
            step(0, 0)
            step(1, 1)
            with dve.Fori(0, B - 1) as b:
                with dve.Fori(0, HEADS // 2 - 1) as j:
                    n = b * HEADS + j * 2 + 2
                    step(n, 0)
                    step(n + 1, 1)
                n = b * HEADS + HEADS
                step(n, 0, post={"first": lambda: post_norms(b, b), "last": lambda: post_fused(b, b)})
                step(n + 1, 1, post={"first": lambda: post_probs(b, b), "middle": lambda: post_probsT(b, b),
                                     "turn": lambda: post_oT(b, b), "last": lambda: post_y(b, b)})
            with dve.Fori(0, HEADS // 2 - 2) as j:
                n = j * 2 + ((B - 1) * HEADS + 2)
                step(n, 0)
                step(n + 1, 1)
            early = range(HEADS - LATE)
            late = range(HEADS - LATE, HEADS)
            step(BH - 2, 0, maxima=False, post={"first": lambda: post_norms(B - 1, B - 1, early)})
            post_fused(B - 1, B - 1, early)
            post_probs(B - 1, B - 1, early)
            for stage in (post_norms, post_fused, post_probs):
                stage(B, B - 1, late)
            for stage in (post_probsT, post_oT, post_y):
                stage(B, B - 1)

        @block.tensor
        def _(pe):
            def keys(b, i):
                c, mg = divmod(i, MG)
                pe.wait_ge(pro_dve, DVE_AT["cols", b, c])
                if i >= 2:
                    pe.wait_ge(pro_dve, DVE_AT["k", b, i - 2])
                elif b == 1:
                    pe.wait_ge(pro_dve, DVE_AT["q", mg])
                elif b >= 2:
                    pe.wait_ge(pro_dve, DVE_AT["k", b - 1, i + 2])
                for a in range(2):
                    cols = slice((2 * c + a) * MC, (2 * c + a + 1) * MC)
                    terms = [(e, w, x_) for e in range(NE) for w, x_ in ((0, 0), (0, 1), (1, 0))]
                    for t, (e, w, x_) in enumerate(terms):
                        last = nc.tensor.matmul(sc_ps[mg][0:CG, a, 0:MC], wk_sb[:, w, e, mg * CG:(mg + 1) * CG],
                                                cT[b % 2][x_][:, e, cols], start=(t == 0), stop=(t == len(terms) - 1))
                return last

            def values(b, i):
                pe.wait_ge(pro_dve, DVE_AT["cols", b, 1])
                pe.wait_ge(pro_dve, DVE_AT["unit", b])
                if i >= 2:
                    pe.wait_ge(pro_dve, DVE_AT["v", b, i - 2])
                else:
                    pe.wait_ge(pro_dve, DVE_AT["v", b - 1, V_LAST - i] if b else DVE_AT["ipv", i])
                s0, k, rows, dst = v_use(i)
                for s in range(s0, s0 + k):
                    t0, n = slot_token(s)
                    terms = [(e, w, x_) for e in range(NE) for x_, w in ((0, 0), (0, 1), (1, 0))]
                    for t, (e, w, x_) in enumerate(terms):
                        last = nc.tensor.matmul(dst[:, s - s0, :], cT[b % 2][x_][:, e, t0:t0 + n],
                                                wv_sb[:, b % 2, w, e, :], start=(t == 0), stop=(t == len(terms) - 1))
                return last

            def norms():
                pe.wait_ge(dve_init, 2)
                for e in range(NE):
                    last = nc.tensor.matmul(max_ps[:, 0, 0:B * IP], ones_sb[:], ip_sq[:, e, :], start=(e == 0),
                                            stop=(e == NE - 1))
                return last

            def ip_keys():
                for mg in range(MG):
                    for e in range(NE):
                        last = nc.tensor.matmul(max_ps[0:CG, 1, mg * B * IP:(mg + 1) * B * IP],
                                                wkip_sb[:, e, mg * CG:(mg + 1) * CG], ip_cols[:, e, :],
                                                start=(e == 0), stop=(e == NE - 1))
                return last

            def ip_values_of(i):
                for b in (2 * i, 2 * i + 1):
                    for e in range(NE):
                        last = nc.tensor.matmul(val_ps[i][0:HEADS * IP, (b % 2) * C:(b % 2 + 1) * C], ip_rep[:, e, b, :],
                                                wvip_sb[:, e, :], start=(e == 0), stop=(e == NE - 1))
                return last

            def queries(mg):
                pe.wait_ge(q_in, 32)
                pe.wait_ge(pro_dve, DVE_AT["k", 0, 2 + mg])
                for a in range(2):
                    for g in range(MG):
                        last = nc.tensor.matmul(sc_ps[mg][0:CG, a, :], wq_sb[:, g, mg * CG:(mg + 1) * CG],
                                                xT_sb[:, g, a * 512:(a + 1) * 512], start=(g == 0), stop=(g == MG - 1))
                return last

            def ip_scores_of(i):
                pe.wait_ge(pro_act, ACT_AT["q", 1])
                pe.wait_ge(pro_dve, DVE_AT["blocks",])
                for b in (2 * i, 2 * i + 1):
                    for half in range(NH):
                        for mg in range(MG):
                            q0 = b * S + half * P
                            c0 = (((b % 2) * NH + half) * MG + mg) * HG * IP
                            last = nc.tensor.matmul(max_ps[:, i, c0:c0 + HG * IP], qT_sb[:, mg, q0:q0 + P],
                                                    bdk[:, mg, b, :, :].rearrange("p h i -> p (h i)"), start=True,
                                                    stop=True)
                return last

            def max_chunk(m, g, c, par):
                half, chunk = divmod(c, 2)
                if c == 0:
                    pe.wait_ge(kq_in[par], 64 * (g + 1))
                if not isinstance(m, int) or m > 0 or c > 0:
                    pe.wait_ge(max_free, 5 * m + c)
                col = chunk * (MC - 1)
                for r in range(2):
                    last = nc.tensor.matmul(max_ps[:, r, 0:MC], q_sb[64 * r:64 * r + KR, par, half * P:(half + 1) * P],
                                            k_sb[64 * r:64 * r + KR, par, col:col + MC], start=True, stop=True)
                last.then_inc(max_scores, 1)

            def max_turn(m):
                pe.wait_ge(max_parts, 2 * m + 2)
                for half in range(NH):
                    last = nc.tensor.matmul(max_ps[:, 0, half * P:(half + 1) * P], max_cols[:, half, :], ident16[:],
                                            start=True, stop=True)
                last.then_inc(max_rows, 1)

            def score_unit(m, u, par, first=False):
                if u == 0:
                    pe.wait_ge(max_free, 5 * m + 5)
                if not first or u >= 2:
                    pe.wait_ge(exps, UNITS * m + (u - 1))
                s0, k, rows = unit_slots(u)
                for s in ([s0, s0 + 2, s0 + 1, s0 + 3] if k == 4 else [s0]):
                    r, col, n = slot_column(s)
                    at = s - s0
                    last = nc.tensor.matmul(sc_ps[u % 2][0:n, at // 2, (at % 2) * S:(at % 2 + 1) * S],
                                            k_sb[64 * r:64 * r + KR, par, col:col + n], q_max[64 * r:64 * r + KR, :],
                                            start=True, stop=True)
                last.then_inc(scores, 1)

            def value_slot(n, half, s, par):
                rows = slot_token(s)[1]
                if half == 0 and s % 4 == 0:
                    u = s // 4
                    if u % 2 == 0:
                        pe.wait_ge(lo_dve, 2 * n + (u // 2 + 1))
                    else:
                        pe.wait_ge(lo_pool, 2 * n + (u // 2 + 1))
                if half == 0 and s == 0:
                    pe.wait_ge(v_cols, n + 1)
                if s == 0:
                    pe.wait_ge(val_read[half], n)
                hi = p_hi[0:rows, par, s, half * P:(half + 1) * P]
                lo = p_lo[0:rows, par, s, half * P:(half + 1) * P]
                x_hi = aug[0:rows, par, 0, s, 0:W_AUG]
                x_lo = aug[0:rows, par, 1, s, 0:W_AUG]
                acc = val_ps[half][:, 0:W_AUG]
                nc.tensor.matmul(acc, hi, x_hi, start=(s == 0), stop=False)
                nc.tensor.matmul(acc, hi, x_lo, start=False, stop=False)
                last = nc.tensor.matmul(acc, lo, x_hi, start=False, stop=(s == NT - 1))
                if s == NT - 1:
                    last.then_inc(val_done[half], 1)

            def post_turn_probs(b, k=None):
                pe.wait_ge(post_dve, post_base(b if k is None else k) + POST_AT["text"])
                for half in range(NH):
                    last = nc.tensor.transpose(post_ps[0:HEADS * IP, half * P:(half + 1) * P],
                                               probs[:, half, :, :].rearrange("p h i -> p (h i)"), ident32[:])
                last.then_inc(post_pe, 1)

            def post_turn_out(b, k=None):
                pe.wait_ge(post_dve, post_base(b if k is None else k) + POST_AT["probsT"])
                pe.wait_ge(post_ipv, b + 1)
                for g in range(MG):
                    for half in range(NH):
                        dst = post_ps[0:CG, (g * NH + half) * P:(g * NH + half + 1) * P]
                        nc.tensor.matmul(dst, text[:, half, g * CG:(g + 1) * CG], ident32[:], start=True, stop=False)
                        last = nc.tensor.matmul(dst, ip_values_b[:, g * CG:(g + 1) * CG], probsT[:, half, :],
                                                start=False, stop=True)
                last.then_inc(post_pe, 1)

            def post_project(b, k=None):
                pe.wait_ge(post_dve, post_base(b if k is None else k) + POST_AT["oT"])
                for half in range(NH):
                    dst = post_ps[:, half * C:(half + 1) * C]
                    for g in range(MG):
                        nc.tensor.matmul(dst, oT[0:CG, g, half * P:(half + 1) * P], wout_sb[:, g, :], start=(g == 0),
                                         stop=False)
                    last = nc.tensor.matmul(dst, ones_sb[0:1, :], bout_sb[:], start=False, stop=True)
                last.then_inc(post_pe, 1)

            def step(g, par, score=True, maxima=True, post=None, aug_b=None):
                n = g * 2 + par
                post = post or {}
                between = {}
                if score:
                    for place, u in ((0, 0), (1, 1), (6, 2), (11, 3)):
                        between[place] = lambda u=u: score_unit(n + 1, u, 1 - par)
                if maxima:
                    for place, c in ((2, 0), (7, 1), (12, 2), (17, 3)):
                        between[place] = lambda c=c: max_chunk(n + 2, g + 1, c, par)
                    between[22] = lambda: max_turn(n + 2)
                for half in range(NH):
                    for s in range(NT):
                        for i, slots in enumerate(AUG_SLOTS):
                            if aug_b is not None and half == 0 and s == slots.start:
                                pe.wait_ge(aug_in[par][i], 32 * (aug_b + 1))
                        value_slot(n, half, s, par)
                        place = half * NT + s
                        between.get(place, lambda: None)()
                        post.get(place, lambda: None)()

            parts = {"k": keys, "v": values, "norms": norms, "ipk": ip_keys, "ipv": ip_values_of, "q": queries,
                     "ips": ip_scores_of}
            for name in ORDER:
                if name[0] in parts:
                    parts[name[0]](*name[1:]).then_inc(pro_pe, 1)
                if name[0] == "m":
                    if name[1:] == (0, 0):
                        pe.wait_ge(pro_act, ACT_AT["ips", 1])
                    max_chunk(name[1], 0, name[2], name[1])
                if name[0] == "turn":
                    max_turn(name[1])
                if name[0] == "s":
                    if name[1] < 2:
                        pe.wait_ge(pro_dve, DVE_AT["k", B - 1, 2 + name[1]])
                    score_unit(0, name[1], 0, first=True)
            pe.wait_ge(pro_dve, DVE_AT["v", B - 1, V_LAST])
            step(0, 0, aug_b=0)
            step(0, 1, aug_b=0)
            with pe.Fori(0, B - 1) as b:
                with pe.Fori(0, HEADS // 2 - 1) as j:
                    g = b * (HEADS // 2) + j + 1
                    step(g, 0)
                    step(g, 1)
                g = b * (HEADS // 2) + HEADS // 2

                step(g, 0, aug_b=b + 1)
                step(g, 1, aug_b=b + 1, post={
                    13: lambda: post_turn_probs(b), 18: lambda: post_turn_out(b), 24: lambda: post_project(b),
                    25: lambda: pe.wait_ge(post_dve, post_base(b) + POST_AT["y"])})
            with pe.Fori(0, HEADS // 2 - 2) as j:
                g = j + ((B - 1) * (HEADS // 2) + 1)
                step(g, 0)
                step(g, 1)
            step(BH // 2 - 1, 0, maxima=False)
            step(BH // 2 - 1, 1, score=False, maxima=False)
            for stage in (post_turn_probs, post_turn_out, post_project):
                stage(B - 1, B)


def kernel(x, ctx_2048, fside_S_0, L0_xattn_W_q, L0_xattn_W_k, L0_xattn_W_v, L0_xattn_W_k_ip, L0_xattn_W_v_ip,
           L0_xattn_W_out, L0_xattn_b_out):
    import numpy as np
    import concourse.bacc as bacc
    from concourse import mybir as mb
    from concourse.bass_utils import run_bass_kernel_spmd

    x, ctx = np.asarray(x), np.asarray(ctx_2048)
    B, S, C = x.shape
    heads, ip = HEADS, IP
    channel_head = np.arange(C) // DH
    arrays = {
        "x": x,
        "xT": x.reshape(B * S, C).T,
        "ctx": ctx,
        "ctxT": ctx.transpose(0, 2, 1),
        "smask": np.asarray(fside_S_0).reshape(S // P, P).T,
        "Wq": L0_xattn_W_q,
        "Wk": L0_xattn_W_k,
        "Wv": L0_xattn_W_v,
        "Wkip": L0_xattn_W_k_ip,
        "Wvip": L0_xattn_W_v_ip,
        "Wout": L0_xattn_W_out,
        "bout": L0_xattn_b_out,
        "ip_tokens": ctx[:, -ip:].transpose(2, 0, 1).reshape(ctx.shape[2], B * ip),
        "ident": np.eye(P, dtype=np.float32),
        "bdk_mask": (channel_head[:C // 2, None] == np.arange(heads // 2)[None, :]).astype(np.float32),
        "bdv_mask": (np.repeat(np.arange(heads), ip)[:, None] == channel_head[None, :]).astype(np.float32),
    }
    arrays = {f"in_{k}": np.ascontiguousarray(v) for k, v in arrays.items()}
    nc = bacc.Bacc("TRN2", target_bir_lowering=False, num_devices=1)
    args = [nc.dram_tensor(k, v.shape, mb.dt.from_np(v.dtype), kind="ExternalInput").ap() for k, v in arrays.items()]
    out = nc.dram_tensor("out_y", (B, S, C), mb.dt.float32, kind="ExternalOutput").ap()
    xattn(nc, *args, out)
    r = run_bass_kernel_spmd(nc, [arrays], core_ids=[0])
    return r.results[0]["out_y"]
```

```python
from contextlib import ExitStack

import concourse.bass as bass
from concourse import mybir

ALU = mybir.AluOpType
ACT = mybir.ActivationFunctionType
F16 = mybir.dt.float16
F32 = mybir.dt.float32
AX = mybir.AxisListType

P = 128
LN2 = 0.6931471805599453
EPS = 1e-12
SEM_SCALE = 0.5
X_SCALE = 64.0
K_SCALE = 32.0
HEADS = 20
IP = 4
DH = 8


def xattn(nc, x, xT, ctx, ctxT, smask, Wq, Wk, Wv, Wkip, Wvip, Wout, bout, ip_tokens, ident, bdk_mask, bdv_mask, out):
    B, S, C = x.shape
    T = ctx.shape[1] - IP
    E = ctx.shape[2]
    NE = E // P
    NH = S // P
    BH = B * HEADS
    MG = 2
    CG = C // MG
    HG = HEADS // MG
    SOFT = DH ** -0.5
    Q_SCALE = 32.0 * SOFT
    S_SCALE = 2.0 ** -10
    P_SHIFT = 14 * LN2

    NT = (T + P - 1) // P
    TAIL = T - (NT - 1) * P
    G0 = (NT - 1) // 2 * P + TAIL
    GM = (T + 1) // 2
    MC = 400
    G1_FIRST = T - GM
    UNITS = (NT + 3) // 4
    KROWS = 3 * DH
    KR = KROWS + 2
    assert (NT - 1) % 4 == 0 and 2 * MC - 1 == GM and G0 >= GM and T - G0 == (NT - 1) // 2 * P

    STACK = 64 + TAIL
    TAIL_COL = (NT - 1) // 2 * P
    DUP = STACK - TAIL

    def slot_token(slot):
        if slot == NT - 1:
            return (NT - 1) // 2 * P, TAIL
        u, k = divmod(slot, 4)
        return (2 * u + k, 0)[0] * P if k < 2 else G0 + (2 * u + k - 2) * P, P

    def slot_column(slot):
        t0, n = slot_token(slot)
        if slot == NT - 1:
            return 0, TAIL_COL, STACK
        return (0, t0, n) if slot % 4 < 2 else (1, t0 - G1_FIRST, n)

    CG_IP = E
    CG_ONE = E + IP
    CG_V = CG_ONE + 2
    W_AUG = CG_V + DH
    W_RES = W_AUG - E

    k_dram = nc.dram_tensor("k_stacked", (3, BH * DH, T), F16).ap()
    q_dram = nc.dram_tensor("q_stacked", (3, BH * DH, S), F16).ap()

    with ExitStack() as st:
        def sb(name, shape, dt):
            return st.enter_context(nc.sbuf_tensor(name, shape, dt))

        def psum(name, shape, dt):
            return st.enter_context(nc.psum_tensor(name, shape, dt))

        def sem(name):
            return st.enter_context(nc.semaphore(name))

        ctx_parts = sb("ctx_parts", [P, B, 2, NT, CG_V], F16)
        v_parts = sb("v_parts", [P, 2, NT, B * C], F16)
        wout_sb = sb("wout_sb", [CG, MG, C], F32)
        bout_sb = sb("bout_sb", [1, C], F32)
        ones_sb = sb("ones_sb", [P, P], F32)
        ident32 = sb("ident32", [P, P], F32)
        ident16 = sb("ident16", [P, P], F16)
        smask_sb = sb("smask_sb", [P, NH], F32)
        x_sb = sb("x_sb", [P, B * NH, C], F32)
        ip_scores = sb("ip_scores", [P, B, HEADS, NH, IP], F32)
        ip_values = sb("ip_values", [HEADS * IP, B * C], F32)
        heads_out = sb("heads_out", [P, BH, NH, W_RES], F32)
        sem_sq = sb("sem_sq", [P, BH, NH], F32)
        half_pow = sb("half_pow", [P, HEADS * NH], F32)
        k_sb = sb("k_sb", [P, 2, (G0 + DUP) // 2 * 2 + 2], F16)
        q_sb = sb("q_sb", [P, 2, S], F16)
        q_max = sb("q_max", [P, S], F16)
        max_cols = sb("max_cols", [P, NH, P], F16)
        aug = sb("aug", [P, 2, 2, NT, W_AUG], F16)
        p_hi = sb("p_hi", [P, 2, NT, S], F16)
        p_lo = sb("p_lo", [P, 2, NT, S], F16)
        p_32 = sb("p_32", [P, NT, S], F32)
        mx = sb("mx", [P, NH, 2], F32)
        mx1 = sb("mx1", [P, NH], F32)
        den = sb("den", [P, HEADS, NH], F32)
        eps_sq = sb("eps_sq", [P, HEADS, NH], F32)
        guard = sb("guard", [P, HEADS, NH], F32)
        rnorm = sb("rnorm", [P, HEADS, NH], F32)
        rden = sb("rden", [P, HEADS, NH], F32)
        fused = sb("fused", [P, HEADS, NH, IP], F32)
        fmax = sb("fmax", [P, HEADS, NH], F32)
        probs = sb("probs", [P, NH, HEADS, IP], F32)
        text = sb("text", [P, NH, C], F32)
        probsT = sb("probsT", [HEADS * IP, NH, P], F32)
        ip_values_b = sb("ip_values_b", [HEADS * IP, C], F32)
        fsum = sb("fsum", [P, HEADS, NH], F32)
        rsum = sb("rsum", [P, HEADS, NH], F32)
        oT = sb("oT", [P, MG, S], F32)

        max_ps = psum("max_ps", [P, 2, 512], F32)
        sc_ps = [psum(f"sc_ps{i}", [P, 2, 512], F32) for i in range(2)]
        post_ps = sc_ps[1][:, 1, :]
        val_ps = [psum(f"val_ps{i}", [P, 512], F32) for i in range(2)]

        q_in = sem("q_in")
        consts_in = sem("consts_in")
        x_in = sem("x_in")
        ip_in = sem("ip_in")
        wkv_in = [sem("wk_in"), sem("wv_in")]
        c_in = [[sem(f"c_in{b}_{h}") for h in range(2)] for b in range(B)]
        cT_in = [[sem(f"cT_in{b}_{c}") for c in range(2)] for b in range(B)]
        ones_set = sem("ones_set")
        twice = [sem(f"twice{b}") for b in range(B)]
        pro_pe = sem("pro_pe")
        pro_act = sem("pro_act")
        pro_dve = sem("pro_dve")
        pro_pool = sem("pro_pool")
        pool_init = sem("pool_init")
        dve_init = sem("dve_init")
        unit_hi = sem("unit_hi")
        pool_ip = sem("pool_ip")
        post_ipv = sem("post_ipv")
        q_out = sem("q_out")
        k_out = [sem(f"k_out{g}") for g in range(MG)]
        aug_in = [[sem(f"aug_in{par}_{i}") for i in range(2)] for par in range(2)]
        kq_in = [sem(f"kq_in{i}") for i in range(2)]
        max_scores = sem("max_scores")
        max_free = sem("max_free")
        max_parts = sem("max_parts")
        max_one = sem("max_one")
        max_rows = sem("max_rows")
        scores = sem("scores")
        exps = sem("exps")
        lo_dve = sem("lo_dve")
        lo_pool = sem("lo_pool")
        v_cols = sem("v_cols")
        val_done = [sem(f"val_done{i}") for i in range(NH)]
        val_read = [sem(f"val_read{i}") for i in range(NH)]
        post_dve = sem("post_dve")
        post_pool = sem("post_pool")
        post_act = sem("post_act")
        post_pe = sem("post_pe")
        y_out = sem("y_out")

        def view(tensor, start, shape, dt):
            flat = tensor[0:shape[0]]
            size = shape[1] * shape[2] * (2 if dt == F32 else 1)
            flat = flat.rearrange("p a b c -> p (a b c)" if len(flat.shape) == 4 else "p a b c d -> p (a b c d)")
            part = flat[:, start:start + size]
            part = part.bitcast(F32) if dt == F32 else part
            return part.rearrange("p (a b) -> p a b", a=shape[1])

        TALL = T + IP
        W_SCALE = 64.0
        PART = NE * TALL
        c_rows = p_32
        cT_raw = view(aug, 0, [P, NE, TALL], F32)
        kh = view(aug, 2 * NT * W_AUG, [CG, MG, TALL], F16)
        kl = view(aug, 2 * NT * W_AUG + MG * TALL, [CG, MG, TALL], F16)
        cT = [[view(t, part * PART, [P, NE, TALL], F16) for part in range(2)] for t in (p_hi, p_lo)]
        wk_raw = v_parts[:, 0, 0, :].bitcast(F32).rearrange("p (e c) -> p e c", e=NE)
        wv_raw = v_parts[:, 0, 1, :].bitcast(F32).rearrange("p (e c) -> p e c", e=NE)
        xT_sb = heads_out[0:CG].rearrange("p a b c -> p (a b c)")[:, 0:MG * B * S].rearrange("p (g t) -> p g t", g=MG)
        wq_sb = k_sb[0:CG].rearrange("p a b -> p (a b)")[:, 0:2 * MG * C].bitcast(F32).rearrange("p (g c) -> p g c", g=MG)
        qh = x_sb[0:CG].rearrange("p a b -> p (a b)").bitcast(F16)[:, 0:MG * B * S].rearrange("p (g t) -> p g t", g=MG)
        wkip_sb = text[:]
        wvip_sb = oT[:, :, 0:C]
        ql = sb("ql", [CG, MG, B * S], F16)
        qT_sb = sb("qT_sb", [CG, MG, B * S], F32)
        wk_sb = sb("wk_sb", [P, 2, NE, C], F16)
        wv_sb = sb("wv_sb", [P, 2, 2, NE, C + IP], F16)
        bdk_mask_sb = sb("bdk_mask_sb", [CG, HG], F32)
        bdv_mask_sb = sb("bdv_mask_sb", [HEADS * IP, C], F32)
        ip_cols = sb("ip_cols", [P, NE, B * IP], F32)
        ip_sq = sb("ip_sq", [P, NE, B * IP], F32)
        ip_rep = sb("ip_rep", [P, NE, B, HEADS * IP], F32)
        ip_unit = sb("ip_unit", [P, NE, B * IP], F32)
        ip_n2 = sb("ip_n2", [P, B * IP], F32)
        ip_rn = sb("ip_rn", [P, B * IP], F32)
        kipT = sb("kipT", [CG, MG, B * IP], F32)
        bdk = ip_rep[0:CG].rearrange("p e b h -> p (e b h)")[:, 0:MG * B * HG * IP].rearrange(
            "p (g b h i) -> p g b h i", g=MG, b=B, h=HG)

        block = st.enter_context(nc.Block())

        N_CONSTS = 6

        V_PER = 3
        V_USES = (NT + V_PER - 1) // V_PER
        ORDER = """in_cols 0 0, in_cols 0 1, in_ip, in_x, w 0, cols 0 0, cols 0 1, in_cols 1 0, in_cols 1 1, in_rows 0 0,
            k 0 0, w 1, copies, k 0 1, k 0 2, in_consts, norms, ipk, k 0 3, in_rows 0 1, ipv 0, ipv 1, cols 1 0,
            unit 0, blocks, out_k 0 0, out_k 0 1, q 0, v 0 0, in_cols 2 0, unit 1, cols 1 1, v 0 1, scale 0 1,
            rows 0 0, q 1, out_q 0, v 0 2, in_rows 1 0, k 1 0, v 0 3, v 0 4, rows 0 1, out_q 1, in_cols 2 1,
            in_residual, in_head 0,
            ips 0, v 1 0, in_rows 1 1, unit 2, k 1 1, cols 2 0, ips 1, rows 1 0, scale 1 1, v 1 1, in_head 1,
            k 1 2, v 1 2, cols 2 1, rows 1 1, m 0 0, out_k 1 0, in_cols 3 0, k 1 3, v 1 3, out_k 1 1, v 1 4,
            in_rows 2 0, in_cols 3 1,
            k 2 0, v 2 0, unit 3, k 2 1, cols 3 0, rows 2 0, scale 2 1, m 0 1, v 2 1, in_rows 2 1, k 2 2, v 2 2,
            m 0 2, out_k 2 0, cols 3 1, rows 2 1, k 2 3, v 2 3, m 0 3, in_rows 3 0, out_k 2 1, v 2 4,
            in_rows 3 1, twice 0, twice 1, twice 2, in_aug 0,
            k 3 0, v 3 0, turn 0, k 3 1, m 1 0, rows 3 0, scale 3 1, v 3 1, k 3 2, m 1 1, rows 3 1, v 3 2, out_k 3 0,
            k 3 3, m 1 2, out_k 3 1, v 3 3, s 0, m 1 3, v 3 4, twice 3, s 1, s 2, lo 0, s 3, turn 1"""
        ORDER = [tuple(int(w) if w.isdigit() else w for w in step.split()) for step in ORDER.split(",")]

        def tally(order):
            return {name: i + 1 for i, name in enumerate(order)}

        def share(*kinds):
            return tally([step for step in ORDER if step[0] in kinds])

        PE_AT = share("k", "v", "norms", "ipk", "ipv", "q", "ips")
        ACT_AT = share("w", "cols", "rows", "k", "v", "q", "ips")
        DVE_AT = share("w", "cols", "scale", "k", "v", "unit", "norms", "ipk", "ipv", "blocks", "q")
        POOL_AT = share("rows")
        V_LAST = V_USES - 1

        def v_use(i):
            s0 = V_PER * i
            k = min(V_PER, NT - s0)
            rows = P if s0 + k < NT else TAIL
            assert rows == P or k == 1
            return s0, k, rows, val_ps[i % 2][0:rows, 0:k * (C + IP)].rearrange("p (s c) -> p s c", s=k)

        AUG_SLOTS = (slice(0, 6), slice(6, NT))
        ROWS_OF = (slice(0, 6), slice(6, NT))

        POST_AT = tally(["den", "eps", "guard", "rden", "text", "dots", "fused", "fmax", "shifted", "fsum", "rsum",
                         "masked", "probs", "probsT", "oT", "y"])
        POST_DVE = len(POST_AT)
        POST_OWN = POST_AT["probs"]
        EARLY_AT = {"probsT": POST_OWN + 1, "oT": POST_OWN + 2}
        POST_EARLY = POST_OWN + len(EARLY_AT)
        POST_END = POST_DVE * B + POST_EARLY
        IP_ROWS = HG * IP
        LATE = 2

        def unit_slots(u):
            return (4 * u, min(4, NT - 4 * u), P if u < UNITS - 1 else STACK)

        POOL_UNIT = 1

        def lo_count(m, u):
            return (UNITS - 1) * m + (u + 1 if u < POOL_UNIT else u)

        def lo_unit(engine, u, par):
            s0, k, rows = unit_slots(u)
            if u == UNITS - 1:
                return engine.tensor_tensor(p_hi[64:STACK, par, s0, :], p_32[64:STACK, s0, :],
                                            p_hi[64:STACK, par, s0, :], ALU.subtract)
            return engine.tensor_tensor(p_lo[0:rows, par, s0:s0 + k, :], p_32[0:rows, s0:s0 + k, :],
                                        p_hi[0:rows, par, s0:s0 + k, :], ALU.subtract)

        def rows_pieces(b, h):
            full = slice(ROWS_OF[h].start, min(ROWS_OF[h].stop, NT - 1))
            return [(slice(0, P), full)] + ([(slice(0, TAIL), slice(NT - 1, NT))] if h == 1 else [])

        def post_base(k):
            return POST_DVE * (B - 1) + POST_EARLY if isinstance(k, int) and k == B else k * POST_DVE

        @block.sync
        def _(sp):
            def head_load(n, par):
                for g in range(2):
                    cols = slice(0, G0) if g == 0 else slice(G1_FIRST, T)
                    w = G0 if g == 0 else GM
                    sp.dma_start(k_sb[64 * g:64 * g + KROWS, par, 0:w],
                                 k_dram[:, bass.ds(n * DH, DH), cols]).then_inc(kq_in[par], 16)
                    if g == 0:
                        sp.dma_start(k_sb[0:KROWS, par, G0:G0 + DUP],
                                     k_dram[:, bass.ds(n * DH, DH), G0 - DUP:G0]).then_inc(kq_in[par], 16)
                    sp.dma_start(q_sb[64 * g:64 * g + KROWS, par, :],
                                 q_dram[:, bass.ds(n * DH, DH), :]).then_inc(kq_in[par], 16)

            def aug_load(b, par):
                for i, slots in enumerate(AUG_SLOTS):
                    for part in range(2):
                        sp.dma_start(aug[:, par, part, slots, 0:CG_V],
                                     ctx_parts[:, bass.ds(b, 1), part, slots, :].rearrange("p o s c -> p (o s) c")
                                     ).then_inc(aug_in[par][i], 16)

            def rows_load(b, h):
                if b:
                    sp.wait_ge(pro_pool, POOL_AT["rows", b - 1, h])
                elif h == 0:
                    sp.wait_ge(pro_act, ACT_AT["w", 0])
                for s in range(NT)[ROWS_OF[h]][::2]:
                    t0, n = slot_token(s)
                    if n == P:
                        sp.dma_start(c_rows[:, s:s + 2, :], ctx[b, t0:t0 + 2 * P, :].rearrange("(s p) c -> p s c", p=P)
                                     ).then_inc(c_in[b][h], 16)
                    else:
                        sp.dma_start(c_rows[0:n, s, :], ctx[b, t0:t0 + n, :]).then_inc(c_in[b][h], 16)

            def columns_load(b, c):
                if b:
                    sp.wait_ge(pro_dve, DVE_AT["cols", b - 1, c])
                cols = slice(c * 2 * MC, 2 * MC if c == 0 else TALL)
                sp.dma_start(cT_raw[:, :, cols], ctxT[b].rearrange("(e p) t -> p e t", p=P)[:, :, cols]
                             ).then_inc(cT_in[b][c], 16)

            def keys_store(b, mg):
                sp.wait_ge(pro_dve, DVE_AT["k", b, 2 + mg])
                row = b * C + mg * CG
                for r, part in enumerate([kh, kl, kh]):
                    sp.dma_start(k_dram[r, row:row + CG, :], part[:, mg, 0:T]).then_inc(k_out[mg], 16)

            def queries_store(mg):
                sp.wait_ge(pro_dve, DVE_AT["q", mg])
                for r, part in enumerate([qh, qh, ql]):
                    sp.dma_start(q_dram[r].rearrange("(b g c) s -> c g b s", b=B, g=MG)[:, mg, :, :],
                                 part[:, mg, :].rearrange("c (b s) -> c b s", b=B)).then_inc(q_out, 16)

            def residual_load():
                sp.wait_ge(q_out, 16 * 3 * MG)
                sp.dma_start(x_sb[:], x.rearrange("b (h p) c -> p (b h) c", p=P)).then_inc(x_in, 16)

            def first_head_load(n):
                if n == 0:
                    for mg in range(MG):
                        sp.wait_ge(k_out[mg], 16 * 3)
                    sp.wait_ge(q_out, 16 * 3 * MG)
                    sp.wait_ge(pool_init, 2)
                head_load(n, n)

            def first_aug_load(par):
                if par == 0:
                    sp.wait_ge(twice[0], 32)
                    sp.wait_ge(pro_dve, DVE_AT["cols", B - 1, 1])
                else:
                    for mg in range(MG):
                        sp.wait_ge(k_out[mg], 16 * 3 * B)
                aug_load(0, par)

            def ip_weights_load():
                sp.dma_start(wkip_sb, Wkip.rearrange("(e p) n -> p e n", p=P)).then_inc(ip_in, 16)
                sp.dma_start(wvip_sb, Wvip.rearrange("(e p) n -> p e n", p=P)).then_inc(ip_in, 16)

            def queries_load():
                sp.dma_start(xT_sb, xT.rearrange("(g c) t -> c g t", g=MG)).then_inc(q_in, 16)
                sp.dma_start(wq_sb, Wq.rearrange("(g c) n -> c g n", g=MG)).then_inc(q_in, 16)

            def constants_load():
                sp.dma_start(bdk_mask_sb[:], bdk_mask).then_inc(consts_in, 16)
                sp.dma_start(bdv_mask_sb[:], bdv_mask).then_inc(consts_in, 16)
                sp.dma_start(ident32[:], ident).then_inc(consts_in, 16)
                sp.dma_start(wout_sb[:], Wout.rearrange("(g c) n -> c g n", g=MG)).then_inc(consts_in, 16)
                sp.dma_start(bout_sb[:], bout.rearrange("(o c) -> o c", o=1)).then_inc(consts_in, 16)
                sp.dma_start(smask_sb[:], smask).then_inc(consts_in, 16)

            def short_slot_twice(b):
                sp.wait_ge(pro_act, max(ACT_AT["rows", b, 1], ACT_AT["v", b, V_LAST]))
                sp.dma_start(ctx_parts[64:STACK, b, 0, NT - 1, 0:CG_ONE],
                             ctx_parts[0:TAIL, b, 0, NT - 1, 0:CG_ONE]).then_inc(twice[b], 16)
                sp.dma_start(v_parts[64:STACK, 0, NT - 1, b * C:(b + 1) * C],
                             v_parts[0:TAIL, 0, NT - 1, b * C:(b + 1) * C]).then_inc(twice[b], 16)

            parts = {"twice": short_slot_twice, "in_ip": ip_weights_load, "in_x": queries_load, "in_consts": constants_load, "in_rows": rows_load, "in_cols": columns_load, "out_k": keys_store, "out_q": queries_store,
                     "in_residual": residual_load, "in_head": first_head_load, "in_aug": first_aug_load}
            for name in ORDER:
                if name[0] in parts:
                    parts[name[0]](*name[1:])
            sp.wait_ge(scores, UNITS)
            head_load(2, 0)
            first_aug_load(1)
            for b in range(1, B):
                sp.wait_ge(twice[b], 32)

            def step(n, par):
                sp.wait_ge(scores, UNITS * (n + 2))
                head_load(n + 3, 1 - par)

            with sp.Fori(0, B - 1) as b:
                with sp.Fori(0, HEADS // 2 - 1) as j:
                    n = b * HEADS + j * 2
                    step(n, 0)
                    step(n + 1, 1)
                n = b * HEADS + (HEADS - 2)
                step(n, 0)
                sp.wait_ge(val_done[1], n + 1)
                aug_load(b + 1, 0)
                step(n + 1, 1)
                sp.wait_ge(val_done[1], n + 2)
                aug_load(b + 1, 1)
            with sp.Fori(0, HEADS // 2 - 2) as j:
                n = j * 2 + (B - 1) * HEADS
                step(n, 0)
                step(n + 1, 1)
            step(BH - 4, 0)

        @block.gpsimd
        def _(pool):
            nc.gpsimd.memset(ctx_parts[:, :, :, NT - 1, 0:CG_ONE], 0.0)
            nc.gpsimd.memset(v_parts[:, :, NT - 1, :], 0.0)
            nc.gpsimd.memset(q_sb[:], 0.0)
            nc.gpsimd.memset(max_cols[:], 0.0)
            nc.gpsimd.memset(half_pow[:], -0.5)
            nc.gpsimd.memset(ctx_parts[:, :, 0, :, CG_ONE:CG_ONE + 1], X_SCALE)
            nc.gpsimd.memset(ctx_parts[:, :, 0, :, CG_ONE + 1:CG_V], 0.0)
            nc.gpsimd.memset(ctx_parts[:, :, 1, :, CG_ONE:CG_V], 0.0).then_inc(ones_set, 1)
            pool.wait_ge(ones_set, 1)
            nc.gpsimd.memset(ctx_parts[32:64, :, 0, NT - 1, CG_ONE:CG_ONE + 1], 0.0).then_inc(ones_set, 1)
            pool.wait_ge(ones_set, 2)
            nc.gpsimd.memset(ctx_parts[32:TAIL, :, 0, NT - 1, CG_ONE:CG_ONE + 1], X_SCALE).then_inc(pool_init, 1)
            pool.wait_ge(pro_dve, DVE_AT["norms",])
            pool.wait_ge(pool_init, 1)
            nc.gpsimd.tensor_tensor(ip_rn[:], ip_n2[:], half_pow[:, 0:B * IP], ALU.pow).then_inc(pool_ip, 1)
            pool.wait_ge(pool_ip, 1)
            nc.gpsimd.tensor_tensor(ip_unit[:], ip_cols[:], ip_rn[:].unsqueeze(1).to_broadcast([P, NE, B * IP]),
                                    ALU.mult).then_inc(pool_ip, 1)

            def rows_lo(b, h):
                pool.wait_ge(pro_act, ACT_AT["rows", b, h])
                for p_, slots in rows_pieces(b, h):
                    last = nc.gpsimd.tensor_tensor(ctx_parts[p_, b, 1, slots, 0:E], c_rows[p_, slots, :],
                                                   ctx_parts[p_, b, 0, slots, 0:E], ALU.subtract)
                return last

            for name in ORDER:
                if name == ("k", 1, 0):
                    pool.wait_ge(pro_pe, PE_AT["q", 1])
                    nc.gpsimd.memset(k_sb[:], -K_SCALE * 32.0).then_inc(pool_init, 1)
                if name[0] == "rows":
                    rows_lo(*name[1:]).then_inc(pro_pool, 1)

            def values_of(m, par):
                nc.gpsimd.tensor_copy(aug[:, par, :, :, CG_V:W_AUG],
                                      v_parts[:, :, :, bass.ds(m * DH, DH)]).then_inc(v_cols, 1)

            def lo_parts(m, par):
                pool.wait_ge(exps, UNITS * m + (POOL_UNIT + 1))
                lo_unit(nc.gpsimd, POOL_UNIT, par).then_inc(lo_pool, 1)

            def head(m, par, between=lambda: None):
                pool.wait_ge(val_done[1], m - 1)
                values_of(m, par)
                between()
                lo_parts(m, par)

            def post_pow(k, heads):
                g0, g1 = heads.start * NH, heads.stop * NH
                pool.wait_ge(post_dve, post_base(k) + POST_AT["guard"])
                nc.gpsimd.tensor_tensor(rnorm[:].rearrange("p h n -> p (h n)")[:, g0:g1],
                                        guard[:].rearrange("p h n -> p (h n)")[:, g0:g1],
                                        half_pow[:, g0:g1], ALU.pow).then_inc(post_pool, 1)

            def post_values(b):
                nc.gpsimd.tensor_copy(ip_values_b[:], ip_values[:, bass.ds(b * C, C)]).then_inc(post_ipv, 1)

            pool.wait_ge(pro_dve, DVE_AT["cols", B - 1, 1])
            pool.wait_ge(twice[0], 32)
            values_of(0, 0)
            pool.wait_ge(pro_pe, PE_AT["v", B - 1, V_LAST])
            lo_parts(0, 0)
            for mg in range(MG):
                pool.wait_ge(k_out[mg], 16 * 3 * B)
            values_of(1, 1)
            lo_parts(1, 1)
            for b in range(1, B):
                pool.wait_ge(twice[b], 32)
            with pool.Fori(0, B - 1) as b:
                with pool.Fori(0, HEADS // 2 - 1) as j:
                    m = b * HEADS + j * 2 + 2
                    head(m, 0)
                    head(m + 1, 1)
                m = b * HEADS + HEADS
                head(m, 0)
                head(m + 1, 1, between=lambda: post_pow(b, range(HEADS)))
                post_values(b)
            with pool.Fori(0, HEADS // 2 - 2) as j:
                m = j * 2 + ((B - 1) * HEADS + 2)
                head(m, 0)
                head(m + 1, 1)
            head(BH - 2, 0)
            post_values(B - 1)
            head(BH - 1, 1, between=lambda: post_pow(B - 1, range(HEADS - LATE)))
            post_pow(B, range(HEADS - LATE, HEADS))

        @block.scalar
        def _(act):
            act.dma_start(wk_raw, Wk.rearrange("(e p) n -> p e n", p=P)).then_inc(wkv_in[0], 16)
            act.dma_start(wv_raw, Wv.rearrange("(e p) n -> p e n", p=P)).then_inc(wkv_in[1], 16)
            act.dma_start(ip_cols[:], ip_tokens.rearrange("(e p) t -> p e t", p=P)).then_inc(ip_in, 16)
            def weights_hi(i):
                act.wait_ge(wkv_in[i], 16)
                if i == 0:
                    return nc.scalar.activation(wk_sb[:, 0], wk_raw, ACT.Copy, scale=W_SCALE)
                for par in range(2):
                    last = nc.scalar.activation(wv_sb[:, par, 0, :, 0:C], wv_raw, ACT.Copy, scale=W_SCALE)
                return last

            def columns_hi(b, c):
                act.wait_ge(cT_in[b][c], 16)
                if b >= 2:
                    act.wait_ge(pro_pe, PE_AT["v", b - 2, V_LAST])
                cols = slice(c * 2 * MC, 2 * MC if c == 0 else TALL)
                return nc.scalar.activation(cT[b % 2][0][:, :, cols], cT_raw[:, :, cols], ACT.Copy, scale=X_SCALE)

            def rows_hi(b, h):
                if (b, h) == (0, 0):
                    act.wait_ge(pool_init, 1)
                scaled = ("scale", b, h) in DVE_AT
                if scaled:
                    act.wait_ge(pro_dve, DVE_AT["scale", b, h])
                else:
                    act.wait_ge(c_in[b][h], 16 * len(range(NT)[ROWS_OF[h]][::2]))
                for p_, slots in rows_pieces(b, h):
                    last = nc.scalar.activation(ctx_parts[p_, b, 0, slots, 0:E], c_rows[p_, slots, :], ACT.Copy,
                                                scale=1.0 if scaled else X_SCALE)
                    if not scaled:
                        last = nc.scalar.activation(c_rows[p_, slots, :], c_rows[p_, slots, :], ACT.Copy,
                                                    scale=X_SCALE)
                return last

            def key_hi(b, i):
                c, mg = divmod(i, MG)
                act.wait_ge(pro_pe, PE_AT["k", b, i])
                if b >= 1 and c == 0:
                    act.wait_ge(k_out[mg], 16 * 3 * b)
                return nc.scalar.activation(kh[:, mg, 2 * MC * c:2 * MC * (c + 1)].rearrange("p (a t) -> p a t", a=2),
                                            sc_ps[mg][0:CG, :, 0:MC], ACT.Copy, scale=K_SCALE / (X_SCALE * W_SCALE))

            def value_hi(b, i):
                s0, k, rows, src = v_use(i)
                act.wait_ge(pro_pe, PE_AT["v", b, i])
                if (b, i) == (0, 0):
                    act.wait_ge(pro_dve, DVE_AT["w", 1])
                nc.scalar.activation(v_parts[0:rows, 0, s0:s0 + k, b * C:(b + 1) * C], src[:, :, 0:C], ACT.Copy,
                                     scale=1.0 / W_SCALE)
                return nc.scalar.activation(ctx_parts[0:rows, b, 0, s0:s0 + k, CG_IP:CG_ONE], src[:, :, C:C + IP],
                                            ACT.Copy, scale=1.0 / W_SCALE)

            def queries_hi(mg):
                act.wait_ge(pro_pe, PE_AT["q", mg])
                src = sc_ps[mg][0:CG, :, :].rearrange("c a t -> c (a t)")
                nc.scalar.activation(qT_sb[:, mg, :], src, ACT.Copy)
                return nc.scalar.activation(qh[:, mg, :], src, ACT.Copy, scale=Q_SCALE)

            def ip_scores_out(i):
                act.wait_ge(pro_pe, PE_AT["ips", i])
                for b in (2 * i, 2 * i + 1):
                    c0 = (b % 2) * NH * HEADS * IP
                    last = nc.scalar.activation(
                        ip_scores[:, b, :, :, :], max_ps[:, i, c0:c0 + NH * HEADS * IP].rearrange(
                            "p (a h i) -> p h a i", a=NH, h=HEADS), ACT.Copy, scale=SOFT)
                return last

            def exp_unit(m, u, par, first=False):
                act.wait_ge(scores, UNITS * m + (u + 1))
                if not first:
                    if u == POOL_UNIT:
                        act.wait_ge(lo_pool, m)
                    else:
                        act.wait_ge(lo_dve, lo_count(m - 1, u))
                s0, k, rows = unit_slots(u)
                src = sc_ps[u % 2][0:rows, :, :].rearrange("p a t -> p (a t)")[:, 0:k * S]
                nc.scalar.activation(p_32[0:rows, s0:s0 + k, :].rearrange("p s q -> p (s q)"), src, ACT.Exp,
                                     bias=P_SHIFT, scale=S_SCALE)
                nc.scalar.activation(p_hi[0:rows, par, s0:s0 + k, :].rearrange("p s q -> p (s q)"), src, ACT.Exp,
                                     bias=P_SHIFT, scale=S_SCALE).then_inc(exps, 1)

            def read_values(n, half):
                act.wait_ge(val_done[half], n + 1)
                nc.scalar.activation(val_ps[half][:, 0:E], val_ps[half][:, 0:E], ACT.Square,
                                     accum_out=sem_sq[:, bass.ds(n, 1), half])
                nc.scalar.activation(heads_out[:, bass.ds(n, 1), half, :].rearrange("p o c -> p (o c)"),
                                     val_ps[half][:, E:W_AUG], ACT.Copy).then_inc(val_read[half], 1)

            def post_exp(k, heads=range(HEADS)):
                act.wait_ge(post_dve, post_base(k) + POST_AT["shifted"])
                part = fused[:, heads.start:heads.stop].rearrange("p h n i -> p (h n i)")
                nc.scalar.activation(part, part, ACT.Exp).then_inc(post_act, 1)

            def store(b):
                act.wait_ge(post_dve, post_base(b + 1) if not isinstance(b, int) else POST_END)
                act.dma_start(out[bass.ds(b, 1), :, :].rearrange("o (h p) c -> p (o h) c", p=P),
                              x_sb[:, bass.ds(b * NH, NH), :]).then_inc(y_out, 16)

            def step(n, par, has_next=True, post_b=None):
                if has_next:
                    act.wait_ge(val_done[1], n)
                    exp_unit(n + 1, 0, 1 - par)
                if post_b is not None:
                    post_exp(*post_b)
                if has_next:
                    exp_unit(n + 1, 1, 1 - par)
                    exp_unit(n + 1, 2, 1 - par)
                read_values(n, 0)
                if has_next:
                    exp_unit(n + 1, 3, 1 - par)
                read_values(n, 1)

            parts = {"w": weights_hi, "cols": columns_hi, "rows": rows_hi, "k": key_hi, "v": value_hi,
                     "q": queries_hi, "ips": ip_scores_out}
            for name in ORDER:
                if name[0] in parts:
                    parts[name[0]](*name[1:]).then_inc(pro_act, 1)
                if name[0] == "s":
                    if name[1] == 0:
                        act.wait_ge(pro_pool, POOL_AT["rows", B - 1, 1])
                        act.wait_ge(pro_pe, PE_AT["v", B - 2, V_LAST])
                    exp_unit(0, name[1], 0, first=True)
            step(0, 0)
            step(1, 1)
            with act.Fori(0, B - 1) as b:
                with act.Fori(0, HEADS // 2 - 1) as j:
                    n = b * HEADS + j * 2 + 2
                    step(n, 0)
                    step(n + 1, 1)
                n = b * HEADS + HEADS
                step(n, 0)
                step(n + 1, 1, post_b=(b,))
                store(b)
            with act.Fori(0, HEADS // 2 - 2) as j:
                n = j * 2 + ((B - 1) * HEADS + 2)
                step(n, 0)
                step(n + 1, 1)
            step(BH - 2, 0)
            step(BH - 1, 1, has_next=False, post_b=(B - 1, range(HEADS - LATE)))
            post_exp(B, range(HEADS - LATE, HEADS))
            store(B - 1)
            act.wait_ge(y_out, 16 * B)

        @block.vector
        def _(dve):
            def weights_lo(i):
                dve.wait_ge(pro_act, ACT_AT["w", i])
                targets = [(wk_sb[:, 1], wk_raw, wk_sb[:, 0])] if i == 0 else [
                    (wv_sb[:, par, 1, :, 0:C], wv_raw, wv_sb[:, par, 0, :, 0:C]) for par in range(2)]
                for out_, raw, hi in targets:
                    last = nc.vector.scalar_tensor_tensor(out=out_, in0=raw, scalar=W_SCALE, in1=hi, op0=ALU.mult,
                                                          op1=ALU.subtract)
                return last

            def rows_scale(b, h):
                dve.wait_ge(c_in[b][h], 16 * len(range(NT)[ROWS_OF[h]][::2]))
                for p_, slots in rows_pieces(b, h):
                    last = nc.vector.tensor_scalar(c_rows[p_, slots, :], c_rows[p_, slots, :], X_SCALE, None, ALU.mult)
                return last

            def columns_lo(b, c):
                dve.wait_ge(pro_act, ACT_AT["cols", b, c])
                cols = slice(c * 2 * MC, 2 * MC if c == 0 else TALL)
                return nc.vector.scalar_tensor_tensor(out=cT[b % 2][1][:, :, cols], in0=cT_raw[:, :, cols],
                                                      scalar=X_SCALE, in1=cT[b % 2][0][:, :, cols], op0=ALU.mult,
                                                      op1=ALU.subtract)

            def key_lo(b, i):
                c, mg = divmod(i, MG)
                dve.wait_ge(pro_act, ACT_AT["k", b, i])
                cols = slice(2 * MC * c, 2 * MC * (c + 1))
                return nc.vector.scalar_tensor_tensor(
                    out=kl[:, mg, cols].rearrange("p (a t) -> p a t", a=2), in0=sc_ps[mg][0:CG, :, 0:MC],
                    scalar=K_SCALE / (X_SCALE * W_SCALE), in1=kh[:, mg, cols].rearrange("p (a t) -> p a t", a=2),
                    op0=ALU.mult, op1=ALU.subtract)

            def value_lo(b, i):
                s0, k, rows, src = v_use(i)
                dve.wait_ge(pro_act, ACT_AT["v", b, i])
                nc.vector.scalar_tensor_tensor(
                    out=v_parts[0:rows, 1, s0:s0 + k, b * C:(b + 1) * C], in0=src[:, :, 0:C], scalar=1.0 / W_SCALE,
                    in1=v_parts[0:rows, 0, s0:s0 + k, b * C:(b + 1) * C], op0=ALU.mult, op1=ALU.subtract)
                return nc.vector.scalar_tensor_tensor(
                    out=ctx_parts[0:rows, b, 1, s0:s0 + k, CG_IP:CG_ONE], in0=src[:, :, C:C + IP],
                    scalar=1.0 / W_SCALE, in1=ctx_parts[0:rows, b, 0, s0:s0 + k, CG_IP:CG_ONE], op0=ALU.mult,
                    op1=ALU.subtract)

            def unit_columns(b):
                dve.wait_ge(pool_ip, 2)
                if b >= 2:
                    dve.wait_ge(pro_pe, PE_AT["v", b - 2, V_LAST])
                unit = ip_unit[:, :, b * IP:(b + 1) * IP]
                nc.vector.tensor_scalar(wv_sb[:, b % 2, 0, :, C:C + IP], unit, W_SCALE, None,
                                        ALU.mult).then_inc(unit_hi, 1)
                dve.wait_ge(unit_hi, b + 1)
                return nc.vector.scalar_tensor_tensor(out=wv_sb[:, b % 2, 1, :, C:C + IP], in0=unit, scalar=W_SCALE,
                                                      in1=wv_sb[:, b % 2, 0, :, C:C + IP], op0=ALU.mult,
                                                      op1=ALU.subtract)

            def norms():
                dve.wait_ge(pro_pe, PE_AT["norms",])
                return nc.vector.tensor_scalar(ip_n2[:], max_ps[:, 0, 0:B * IP], EPS * EPS, None, ALU.max)

            def ip_keys():
                dve.wait_ge(pro_pe, PE_AT["ipk",])
                return nc.vector.tensor_copy(kipT[:], max_ps[0:CG, 1, 0:MG * B * IP].rearrange("p (g i) -> p g i", g=MG))

            def ip_values_out(i):
                dve.wait_ge(pro_pe, PE_AT["ipv", i])
                for b in (2 * i, 2 * i + 1):
                    last = nc.vector.tensor_tensor(ip_values[:, b * C:(b + 1) * C],
                                                   val_ps[i][0:HEADS * IP, (b % 2) * C:(b % 2 + 1) * C],
                                                   bdv_mask_sb[:], ALU.mult)
                return last

            def blocks():
                dve.wait_ge(pro_dve, DVE_AT["ipk",])
                for g in range(MG):
                    last = nc.vector.tensor_tensor(
                        bdk[:, g], kipT[:, g, :].rearrange("p (b i) -> p b i", b=B).unsqueeze(2).to_broadcast(
                            [CG, B, HG, IP]),
                        bdk_mask_sb[:].unsqueeze(1).unsqueeze(3).to_broadcast([CG, B, HG, IP]), ALU.mult)
                return last

            def queries_lo(mg):
                dve.wait_ge(pro_act, ACT_AT["q", mg])
                return nc.vector.scalar_tensor_tensor(
                    out=ql[:, mg, :], in0=sc_ps[mg][0:CG, :, :].rearrange("c a t -> c (a t)"), scalar=Q_SCALE,
                    in1=qh[:, mg, :], op0=ALU.mult, op1=ALU.subtract)

            def chunk_max(m, c):
                dve.wait_ge(max_scores, 4 * m + (c + 1))
                nc.vector.tensor_reduce(mx[:, c // 2, c % 2:c % 2 + 1], max_ps[:, :, 0:MC], AX.XY,
                                        ALU.max).then_inc(max_free, 1)

            part_cols = max_cols[:].rearrange("p n (g c) -> p n g c", g=2)

            def max_parts_out(m):
                dve.wait_ge(max_free, 5 * m + 4)
                nc.vector.tensor_tensor(mx1[:], mx[:, :, 0], mx[:, :, 1], ALU.max).then_inc(max_one, 1)
                dve.wait_ge(max_one, m + 1)
                nc.vector.tensor_scalar(part_cols[:, :, :, KROWS], mx1[:].unsqueeze(2).to_broadcast([P, NH, 2]),
                                        S_SCALE, None, ALU.mult).then_inc(max_parts, 1)
                dve.wait_ge(max_parts, 2 * m + 1)
                nc.vector.scalar_tensor_tensor(out=part_cols[:, :, :, KROWS + 1],
                                               in0=mx1[:].unsqueeze(2).to_broadcast([P, NH, 2]), scalar=S_SCALE,
                                               in1=part_cols[:, :, :, KROWS], op0=ALU.mult,
                                               op1=ALU.subtract).then_inc(max_parts, 1)

            def max_to_rows(m, par, first=False):
                dve.wait_ge(max_rows, m + 1)
                if not first:
                    dve.wait_ge(scores, UNITS * m)
                nc.vector.tensor_tensor(q_max[:], q_sb[:, par, :], max_ps[:, 0, 0:S], ALU.add).then_inc(max_free, 1)

            def lo_parts(m, u, par):
                dve.wait_ge(exps, UNITS * m + (u + 1))
                lo_unit(nc.vector, u, par).then_inc(lo_dve, 1)

            def post_step(k, name, instruction, at=POST_AT):
                instruction.then_inc(post_dve, 1)
                dve.wait_ge(post_dve, post_base(k) + at[name])

            def post_norms(k, b, heads=range(HEADS)):
                h0, h = heads.start, len(heads)

                def flat(t):
                    return t[:, h0:h0 + h].rearrange("p h n -> p (h n)")

                dve.wait_ge(val_read[1], b * HEADS + (h0 + h))
                first = b * HEADS + h0
                post_step(k, "den", nc.vector.tensor_scalar(
                    flat(den), heads_out[:, bass.ds(first, h), :, IP:IP + 1].rearrange("p h n c -> p (h n c)"), 1.0,
                    None, ALU.mult))
                post_step(k, "eps", nc.vector.scalar_tensor_tensor(out=flat(eps_sq), in0=flat(den), scalar=EPS * EPS,
                                                                   in1=flat(den), op0=ALU.mult, op1=ALU.mult))
                post_step(k, "guard", nc.vector.tensor_tensor(
                    flat(guard), flat(eps_sq), sem_sq[:, bass.ds(first, h), :].rearrange("p h n -> p (h n)"),
                    ALU.max))
                post_step(k, "rden", nc.vector.reciprocal(flat(rden), flat(den)))
                post_step(k, "text", nc.vector.tensor_tensor(
                    text[:, :, h0 * DH:(h0 + h) * DH].rearrange("p n (h d) -> p h n d", d=DH),
                    heads_out[:, bass.ds(b * HEADS + h0, h), :, CG_V - E:W_RES],
                    rden[:, h0:h0 + h].unsqueeze(3).to_broadcast([P, h, NH, DH]), ALU.mult))

            def post_fused(k, b, heads=range(HEADS)):
                h0, h = heads.start, len(heads)
                part = fused[:, h0:h0 + h]
                groups = part.rearrange("p h n i -> p (h n) i")

                def over_ip(t):
                    return t[:, h0:h0 + h].rearrange("p h n -> p (h n)").unsqueeze(2).to_broadcast([P, h * NH, IP])

                dve.wait_ge(post_pool, k + 1)
                post_step(k, "dots", nc.vector.tensor_tensor(
                    groups, heads_out[:, bass.ds(b * HEADS + h0, h), :, 0:IP].rearrange("p h n c -> p (h n) c"),
                    over_ip(rnorm), ALU.mult))
                post_step(k, "fused", nc.vector.scalar_tensor_tensor(
                    out=part.rearrange("p h n i -> p (h n i)"), in0=part.rearrange("p h n i -> p (h n i)"),
                    scalar=SEM_SCALE,
                    in1=ip_scores[:, bass.ds(b, 1), h0:h0 + h, :, :].rearrange("p o h n i -> p (o h n i)"),
                    op0=ALU.mult, op1=ALU.add))
                post_step(k, "fmax", nc.vector.tensor_reduce(
                    fmax[:, h0:h0 + h].rearrange("p h n -> p (h n)"), groups, AX.X, ALU.max))
                post_step(k, "shifted", nc.vector.tensor_tensor(groups, groups, over_ip(fmax), ALU.subtract))

            def post_probs(k, b, heads=range(HEADS)):
                h0, h = heads.start, len(heads)
                part = fused[:, h0:h0 + h]
                dve.wait_ge(post_act, k + 1)
                sums = rsum[:, h0:h0 + h]
                flat_sums = sums.rearrange("p h n -> p (h n)")
                flat_fsum = fsum[:, h0:h0 + h].rearrange("p h n -> p (h n)")
                post_step(k, "fsum", nc.vector.tensor_reduce(flat_fsum, part.rearrange("p h n i -> p (h n) i"), AX.X,
                                                             ALU.add))
                post_step(k, "rsum", nc.vector.reciprocal(flat_sums, flat_fsum))
                post_step(k, "masked", nc.vector.tensor_tensor(
                    sums, sums, smask_sb[:].unsqueeze(1).to_broadcast([P, h, NH]), ALU.mult))
                post_step(k, "probs", nc.vector.tensor_tensor(
                    probs[:, :, h0:h0 + h, :].rearrange("p n h i -> p h n i"), part,
                    sums.unsqueeze(3).to_broadcast([P, h, NH, IP]), ALU.mult))

            def post_probsT(k, products):
                dve.wait_ge(post_pe, products + 1)
                post_step(k, "probsT", nc.vector.tensor_copy(probsT[:].rearrange("p n s -> p (n s)"),
                                                             post_ps[0:HEADS * IP, 0:S]))

            def post_oT(k, products):
                dve.wait_ge(post_pe, products + 2)
                post_step(k, "oT", nc.vector.tensor_copy(oT[0:CG].rearrange("p g s -> p (g s)"),
                                                         post_ps[0:CG, 0:MG * S]))

            def post_y(k, b, products, y_ps=post_ps[:, 0:NH * C].rearrange("p (n c) -> p n c", n=NH)):
                x_rows = x_sb[:, bass.ds(b * NH, NH), :]
                dve.wait_ge(post_pe, products + 3)
                post_step(k, "y", nc.vector.tensor_tensor(x_rows, y_ps, x_rows, ALU.add))

            def post_group(g, k, at):
                rows = IP_ROWS if g == 0 else HEADS * IP
                dve.wait_ge(post_pe, 3 * (B - 1) + 3 * g + 1)
                post_step(k, "probsT", nc.vector.tensor_copy(probsT[0:rows].rearrange("p n s -> p (n s)"),
                                                             post_ps[0:rows, 0:S]), at)
                dve.wait_ge(post_pe, 3 * (B - 1) + 3 * g + 2)
                post_step(k, "oT", nc.vector.tensor_copy(oT[0:CG, g, :], post_ps[0:CG, g * S:(g + 1) * S]), at)

            def step(n, par, maxima=True, post=None):
                post = post or {}

                def place(name):
                    post.get(name, lambda: None)()

                if maxima:
                    chunk_max(n + 2, 0)
                place("first")
                if maxima:
                    chunk_max(n + 2, 1)
                lo_parts(n + 1, 0, 1 - par)
                place("second")
                if maxima:
                    chunk_max(n + 2, 2)
                place("third")
                lo_parts(n + 1, 2, 1 - par)
                if maxima:
                    chunk_max(n + 2, 3)
                    max_parts_out(n + 2)
                lo_parts(n + 1, 3, 1 - par)
                place("fourth")
                if maxima:
                    max_to_rows(n + 2, par)
                place("last")

            nc.vector.memset(ones_sb[:], 1.0).then_inc(dve_init, 1)
            parts = {"w": weights_lo, "cols": columns_lo, "scale": rows_scale, "k": key_lo, "v": value_lo,
                     "unit": unit_columns, "norms": norms, "ipk": ip_keys, "ipv": ip_values_out, "blocks": blocks,
                     "q": queries_lo}
            for name in ORDER:
                if name == ("copies",):
                    dve.wait_ge(ip_in, 48)
                    for e in range(NE):
                        nc.vector.tensor_copy(
                            ip_rep[:, e, :, :].rearrange("p b (h i) -> p b h i", h=HEADS),
                            ip_cols[:, e, :].rearrange("p (b i) -> p b i", b=B).unsqueeze(2).to_broadcast([P, B, HEADS, IP]))
                    nc.vector.tensor_tensor(ip_sq[:], ip_cols[:], ip_cols[:], ALU.mult).then_inc(dve_init, 1)
                if name == ("ipv", 0):
                    dve.wait_ge(consts_in, 16 * N_CONSTS)
                    nc.vector.tensor_copy(ident16[:], ident32[:]).then_inc(dve_init, 1)
                if name[0] in parts:
                    parts[name[0]](*name[1:]).then_inc(pro_dve, 1)
                if name[0] == "m":
                    chunk_max(*name[1:])
                if name[0] == "lo":
                    lo_parts(0, name[1], 0)
                if name[0] == "turn":
                    dve.wait_ge(pool_init, 2)
                    max_parts_out(name[1])
                    max_to_rows(name[1], name[1], first=(name[1] == 0))
            lo_parts(0, 2, 0)
            lo_parts(0, 3, 0)
            dve.wait_ge(x_in, 16)
            step(0, 0)
            step(1, 1)
            with dve.Fori(0, B - 1) as b:
                with dve.Fori(0, HEADS // 2 - 1) as j:
                    n = b * HEADS + j * 2 + 2
                    step(n, 0)
                    step(n + 1, 1)
                n = b * HEADS + HEADS
                step(n, 0, post={"first": lambda: post_norms(b, b), "last": lambda: post_fused(b, b)})
                step(n + 1, 1, post={"first": lambda: post_probs(b, b), "second": lambda: post_probsT(b, 3 * b),
                                     "third": lambda: post_oT(b, 3 * b), "fourth": lambda: post_y(b, b, 3 * b)})
            with dve.Fori(0, HEADS // 2 - 2) as j:
                n = j * 2 + ((B - 1) * HEADS + 2)
                step(n, 0)
                step(n + 1, 1)
            early = range(HEADS - LATE)
            late = range(HEADS - LATE, HEADS)
            step(BH - 2, 0, maxima=False, post={"first": lambda: post_norms(B - 1, B - 1, early)})
            post_fused(B - 1, B - 1, early)
            post_probs(B - 1, B - 1, early)
            post_group(0, B - 1, EARLY_AT)
            for stage in (post_norms, post_fused, post_probs):
                stage(B, B - 1, late)
            post_group(1, B, POST_AT)
            post_y(B, B - 1, 3 * B, max_ps[:, :, 0:C])

        @block.tensor
        def _(pe):
            def keys(b, i):
                c, mg = divmod(i, MG)
                pe.wait_ge(pro_dve, DVE_AT["cols", b, c])
                if i >= 2:
                    pe.wait_ge(pro_dve, DVE_AT["k", b, i - 2])
                elif b == 1:
                    pe.wait_ge(pro_dve, DVE_AT["q", mg])
                elif b >= 2:
                    pe.wait_ge(pro_dve, DVE_AT["k", b - 1, i + 2])
                for a in range(2):
                    cols = slice((2 * c + a) * MC, (2 * c + a + 1) * MC)
                    terms = [(e, w, x_) for e in range(NE) for w, x_ in ((0, 0), (0, 1), (1, 0))]
                    for t, (e, w, x_) in enumerate(terms):
                        last = nc.tensor.matmul(sc_ps[mg][0:CG, a, 0:MC], wk_sb[:, w, e, mg * CG:(mg + 1) * CG],
                                                cT[b % 2][x_][:, e, cols], start=(t == 0), stop=(t == len(terms) - 1))
                return last

            def values(b, i):
                pe.wait_ge(pro_dve, DVE_AT["cols", b, 1])
                pe.wait_ge(pro_dve, DVE_AT["unit", b])
                if i >= 2:
                    pe.wait_ge(pro_dve, DVE_AT["v", b, i - 2])
                else:
                    pe.wait_ge(pro_dve, DVE_AT["v", b - 1, V_LAST - i] if b else DVE_AT["ipv", i])
                s0, k, rows, dst = v_use(i)
                for s in range(s0, s0 + k):
                    t0, n = slot_token(s)
                    terms = [(e, w, x_) for e in range(NE) for x_, w in ((0, 0), (0, 1), (1, 0))]
                    for t, (e, w, x_) in enumerate(terms):
                        last = nc.tensor.matmul(dst[:, s - s0, :], cT[b % 2][x_][:, e, t0:t0 + n],
                                                wv_sb[:, b % 2, w, e, :], start=(t == 0), stop=(t == len(terms) - 1))
                return last

            def norms():
                pe.wait_ge(dve_init, 2)
                for e in range(NE):
                    last = nc.tensor.matmul(max_ps[:, 0, 0:B * IP], ones_sb[:], ip_sq[:, e, :], start=(e == 0),
                                            stop=(e == NE - 1))
                return last

            def ip_keys():
                for mg in range(MG):
                    for e in range(NE):
                        last = nc.tensor.matmul(max_ps[0:CG, 1, mg * B * IP:(mg + 1) * B * IP],
                                                wkip_sb[:, e, mg * CG:(mg + 1) * CG], ip_cols[:, e, :],
                                                start=(e == 0), stop=(e == NE - 1))
                return last

            def ip_values_of(i):
                for b in (2 * i, 2 * i + 1):
                    for e in range(NE):
                        last = nc.tensor.matmul(val_ps[i][0:HEADS * IP, (b % 2) * C:(b % 2 + 1) * C], ip_rep[:, e, b, :],
                                                wvip_sb[:, e, :], start=(e == 0), stop=(e == NE - 1))
                return last

            def queries(mg):
                pe.wait_ge(q_in, 32)
                pe.wait_ge(pro_dve, DVE_AT["k", 0, 2 + mg])
                for a in range(2):
                    for g in range(MG):
                        last = nc.tensor.matmul(sc_ps[mg][0:CG, a, :], wq_sb[:, g, mg * CG:(mg + 1) * CG],
                                                xT_sb[:, g, a * 512:(a + 1) * 512], start=(g == 0), stop=(g == MG - 1))
                return last

            def ip_scores_of(i):
                pe.wait_ge(pro_act, ACT_AT["q", 1])
                pe.wait_ge(pro_dve, DVE_AT["blocks",])
                for b in (2 * i, 2 * i + 1):
                    for half in range(NH):
                        for mg in range(MG):
                            q0 = b * S + half * P
                            c0 = (((b % 2) * NH + half) * MG + mg) * HG * IP
                            last = nc.tensor.matmul(max_ps[:, i, c0:c0 + HG * IP], qT_sb[:, mg, q0:q0 + P],
                                                    bdk[:, mg, b, :, :].rearrange("p h i -> p (h i)"), start=True,
                                                    stop=True)
                return last

            def max_chunk(m, g, c, par):
                half, chunk = divmod(c, 2)
                if c == 0:
                    pe.wait_ge(kq_in[par], 80 * (g + 1))
                if not isinstance(m, int) or m > 0 or c > 0:
                    pe.wait_ge(max_free, 5 * m + c)
                col = chunk * (MC - 1)
                for r in range(2):
                    last = nc.tensor.matmul(max_ps[:, r, 0:MC], q_sb[64 * r:64 * r + KR, par, half * P:(half + 1) * P],
                                            k_sb[64 * r:64 * r + KR, par, col:col + MC], start=True, stop=True)
                last.then_inc(max_scores, 1)

            def max_turn(m):
                pe.wait_ge(max_parts, 2 * m + 2)
                for half in range(NH):
                    last = nc.tensor.matmul(max_ps[:, 0, half * P:(half + 1) * P], max_cols[:, half, :], ident16[:],
                                            start=True, stop=True)
                last.then_inc(max_rows, 1)

            def score_unit(m, u, par, first=False):
                if u == 0:
                    pe.wait_ge(max_free, 5 * m + 5)
                if not first or u >= 2:
                    pe.wait_ge(exps, UNITS * m + (u - 1))
                s0, k, rows = unit_slots(u)
                for s in ([s0, s0 + 2, s0 + 1, s0 + 3] if k == 4 else [s0]):
                    r, col, n = slot_column(s)
                    at = s - s0
                    last = nc.tensor.matmul(sc_ps[u % 2][0:n, at // 2, (at % 2) * S:(at % 2 + 1) * S],
                                            k_sb[64 * r:64 * r + KR, par, col:col + n], q_max[64 * r:64 * r + KR, :],
                                            start=True, stop=True)
                last.then_inc(scores, 1)

            def value_slot(n, half, s, par):
                rows, lower = (P, P) if s < NT - 1 else (STACK, TAIL)
                if half == 0 and s % 4 == 0:
                    u = s // 4
                    if u == POOL_UNIT:
                        pe.wait_ge(lo_pool, n + 1)
                    else:
                        pe.wait_ge(lo_dve, lo_count(n, u))
                if half == 0 and s == 0:
                    pe.wait_ge(v_cols, n + 1)
                if s == 0:
                    pe.wait_ge(val_read[half], n)
                hi = p_hi[0:rows, par, s, half * P:(half + 1) * P]
                x_hi = aug[0:rows, par, 0, s, 0:W_AUG]
                x_lo = aug[0:lower, par, 1, s, 0:W_AUG]
                acc = val_ps[half][:, 0:W_AUG]
                nc.tensor.matmul(acc, hi, x_hi, start=(s == 0), stop=False)
                last = nc.tensor.matmul(acc, hi[0:lower], x_lo, start=False, stop=(s == NT - 1))
                if s < NT - 1:
                    nc.tensor.matmul(acc, p_lo[:, par, s, half * P:(half + 1) * P], x_hi, start=False, stop=False)
                else:
                    last.then_inc(val_done[half], 1)

            def post_turn_probs(ready, rows=HEADS * IP):
                pe.wait_ge(post_dve, ready)
                for half in range(NH):
                    last = nc.tensor.transpose(post_ps[0:rows, half * P:(half + 1) * P],
                                               probs[:, half, 0:rows // IP, :].rearrange("p h i -> p (h i)"), ident32[:])
                last.then_inc(post_pe, 1)

            def post_turn_out(ready, b, groups=range(MG), rows=HEADS * IP):
                pe.wait_ge(post_dve, ready)
                pe.wait_ge(post_ipv, b + 1)
                for g in groups:
                    for half in range(NH):
                        dst = post_ps[0:CG, (g * NH + half) * P:(g * NH + half + 1) * P]
                        nc.tensor.matmul(dst, text[:, half, g * CG:(g + 1) * CG], ident32[:], start=True, stop=False)
                        last = nc.tensor.matmul(dst, ip_values_b[0:rows, g * CG:(g + 1) * CG], probsT[0:rows, half, :],
                                                start=False, stop=True)
                last.then_inc(post_pe, 1)

            def post_project(ready, groups=range(MG), y_ps=[post_ps[:, half * C:(half + 1) * C] for half in range(NH)]):
                pe.wait_ge(post_dve, ready)
                for half in range(NH):
                    for g in groups:
                        last = nc.tensor.matmul(y_ps[half], oT[0:CG, g, half * P:(half + 1) * P], wout_sb[:, g, :],
                                                start=(g == 0), stop=False)
                    if MG - 1 in groups:
                        last = nc.tensor.matmul(y_ps[half], ones_sb[0:1, :], bout_sb[:], start=False, stop=True)
                last.then_inc(post_pe, 1)

            def step(g, par, score=True, maxima=True, post=None, aug_b=None,
                     chunks_at=(2, 7, 12, 17, 23)):
                n = g * 2 + par
                post = post or {}
                between = {}
                if score:
                    for place, u in ((0, 0), (1, 1), (6, 2), (11, 3)):
                        between[place] = lambda u=u: score_unit(n + 1, u, 1 - par)
                if maxima:
                    for c in range(4):
                        between[chunks_at[c]] = lambda c=c: max_chunk(n + 2, g + 1, c, par)
                    between[chunks_at[4]] = lambda: max_turn(n + 2)
                for half in range(NH):
                    for s in range(NT):
                        for i, slots in enumerate(AUG_SLOTS):
                            if aug_b is not None and half == 0 and s == slots.start:
                                pe.wait_ge(aug_in[par][i], 32 * (aug_b + 1))
                        value_slot(n, half, s, par)
                        place = half * NT + s
                        between.get(place, lambda: None)()
                        post.get(place, lambda: None)()

            parts = {"k": keys, "v": values, "norms": norms, "ipk": ip_keys, "ipv": ip_values_of, "q": queries,
                     "ips": ip_scores_of}
            for name in ORDER:
                if name[0] in parts:
                    parts[name[0]](*name[1:]).then_inc(pro_pe, 1)
                if name[0] == "m":
                    if name[1:] == (0, 0):
                        pe.wait_ge(pro_act, ACT_AT["ips", 1])
                    max_chunk(name[1], 0, name[2], name[1])
                if name[0] == "turn":
                    max_turn(name[1])
                if name[0] == "s":
                    if name[1] < 2:
                        pe.wait_ge(pro_dve, DVE_AT["k", B - 1, 2 + name[1]])
                    score_unit(0, name[1], 0, first=True)
            pe.wait_ge(pro_dve, DVE_AT["v", B - 1, V_LAST])
            step(0, 0, aug_b=0, chunks_at=(8, 13, 17, 21, 25))
            step(0, 1, aug_b=0)
            with pe.Fori(0, B - 1) as b:
                with pe.Fori(0, HEADS // 2 - 1) as j:
                    g = b * (HEADS // 2) + j + 1
                    step(g, 0)
                    step(g, 1)
                g = b * (HEADS // 2) + HEADS // 2

                step(g, 0, aug_b=b + 1)
                step(g, 1, aug_b=b + 1, post={
                    8: lambda: (pe.wait_ge(exps, UNITS * (g * 2 + 2) + 2),
                                post_turn_probs(post_base(b) + POST_AT["probs"])),
                    13: lambda: post_turn_out(post_base(b) + POST_AT["probsT"], b),
                    18: lambda: post_project(post_base(b) + POST_AT["oT"]),
                    25: lambda: pe.wait_ge(post_dve, post_base(b) + POST_AT["y"])})
            with pe.Fori(0, HEADS // 2 - 2) as j:
                g = j + ((B - 1) * (HEADS // 2) + 1)
                step(g, 0)
                step(g, 1)
            step(BH // 2 - 1, 0, maxima=False)
            y_ps = [max_ps[:, half, 0:C] for half in range(NH)]
            early, late = post_base(B - 1), post_base(B)
            step(BH // 2 - 1, 1, score=False, maxima=False, post={
                15: lambda: post_turn_probs(early + POST_OWN, rows=IP_ROWS),
                19: lambda: post_turn_out(early + EARLY_AT["probsT"], B - 1, groups=[0], rows=IP_ROWS),
                23: lambda: post_project(early + EARLY_AT["oT"], groups=[0], y_ps=y_ps)})
            post_turn_probs(late + POST_AT["probs"])
            post_turn_out(late + POST_AT["probsT"], B - 1, groups=[1])
            post_project(late + POST_AT["oT"], groups=[1], y_ps=y_ps)


def kernel(x, ctx_2048, fside_S_0, L0_xattn_W_q, L0_xattn_W_k, L0_xattn_W_v, L0_xattn_W_k_ip, L0_xattn_W_v_ip,
           L0_xattn_W_out, L0_xattn_b_out):
    import numpy as np
    import concourse.bacc as bacc
    from concourse import mybir as mb
    from concourse.bass_utils import run_bass_kernel_spmd

    x, ctx = np.asarray(x), np.asarray(ctx_2048)
    B, S, C = x.shape
    heads, ip = HEADS, IP
    channel_head = np.arange(C) // DH
    arrays = {
        "x": x,
        "xT": x.reshape(B * S, C).T,
        "ctx": ctx,
        "ctxT": ctx.transpose(0, 2, 1),
        "smask": np.asarray(fside_S_0).reshape(S // P, P).T,
        "Wq": L0_xattn_W_q,
        "Wk": L0_xattn_W_k,
        "Wv": L0_xattn_W_v,
        "Wkip": L0_xattn_W_k_ip,
        "Wvip": L0_xattn_W_v_ip,
        "Wout": L0_xattn_W_out,
        "bout": L0_xattn_b_out,
        "ip_tokens": ctx[:, -ip:].transpose(2, 0, 1).reshape(ctx.shape[2], B * ip),
        "ident": np.eye(P, dtype=np.float32),
        "bdk_mask": (channel_head[:C // 2, None] == np.arange(heads // 2)[None, :]).astype(np.float32),
        "bdv_mask": (np.repeat(np.arange(heads), ip)[:, None] == channel_head[None, :]).astype(np.float32),
    }
    arrays = {f"in_{k}": np.ascontiguousarray(v) for k, v in arrays.items()}
    nc = bacc.Bacc("TRN2", target_bir_lowering=False, num_devices=1)
    args = [nc.dram_tensor(k, v.shape, mb.dt.from_np(v.dtype), kind="ExternalInput").ap() for k, v in arrays.items()]
    out = nc.dram_tensor("out_y", (B, S, C), mb.dt.float32, kind="ExternalOutput").ap()
    xattn(nc, *args, out)
    r = run_bass_kernel_spmd(nc, [arrays], core_ids=[0])
    return r.results[0]["out_y"]
```
